# Optimizing a Trainium2 kernel written in Bass

```python
import numpy as np
import jax
import jax.numpy as jnp

def _softmax(x, axis=-1):
    return jax.nn.softmax(x, axis=axis)

def _gelu(x):
    return jax.nn.gelu(x, approximate=True)

def _silu(x):
    return jax.nn.silu(x)

def _sigmoid(x):
    return jax.nn.sigmoid(x)

def _layernorm(x, axis=-1, eps=1e-05):
    m = jnp.mean(x, axis=axis, keepdims=True)
    v = jnp.var(x, axis=axis, keepdims=True)
    return (x - m) / jnp.sqrt(v + eps)

def _scatter_add(tgt, idx, src, axis=0):
    return tgt.at[idx].add(src)

def _segment_sum(src, seg, n):
    return jax.ops.segment_sum(src, seg, n)
kernel_name = 'mk_conv_attn_hybrid_d2_conv_nchw512_r4_2d766f'

def setup_inputs(seed: int=0):
    np.random.seed(seed)
    _w = jnp.asarray

    def _rec_inputs():
        import jax
        import jax.numpy as jnp
        _gk = jax.random.key(seed)
        x = -0.0003929 + 0.9999 * jax.random.normal(jax.random.fold_in(_gk, 1), (8, 128, 16, 16), jnp.float32)
        return x
    x = _rec_inputs()

    def _L0_conv_setup():
        import jax, jax.numpy as jnp
        import numpy as np
        CHANNEL = 128
        INTER = CHANNEL // 2
        key = jax.random.key(seed)
        k0, k1, k2, k3, k4 = jax.random.split(key, 5)
        b, c, h, w = (8, CHANNEL, 16, 16)
        x = jax.random.normal(k0, (b, c, h, w), dtype=jnp.float32)
        s_in = 1.0 / np.sqrt(c)
        s_inter = 1.0 / np.sqrt(INTER)
        w_phi = jax.random.uniform(k1, (INTER, c), jnp.float32, -s_in, s_in)
        w_theta = jax.random.uniform(k2, (INTER, c), jnp.float32, -s_in, s_in)
        w_g = jax.random.uniform(k3, (INTER, c), jnp.float32, -s_in, s_in)
        w_mask = jax.random.uniform(k4, (c, INTER), jnp.float32, -s_inter, s_inter)
        return {'x': x, 'w_phi': w_phi, 'w_theta': w_theta, 'w_g': w_g, 'w_mask': w_mask}
    _L0_conv_all = _L0_conv_setup()
    _L0_conv_in = {k: v for k, v in _L0_conv_all.items() if k in ('w_phi', 'w_theta', 'w_g', 'w_mask')}
    del _L0_conv_all

    def _L1_attn_setup():
        import jax, jax.numpy as jnp
        import numpy as np
        NUM_HEADS = 8
        WINDOW_SIZES = (9, 17)
        key = jax.random.key(seed)
        k1, k2, k3 = jax.random.split(key, 3)
        B, N, C = (2, 512, 128)
        x = jax.random.normal(k1, (B, N, C), dtype=jnp.float32)
        qkv_w = jax.random.normal(k2, (3 * C, C), dtype=jnp.float32) * C ** (-0.5)
        proj_w = jax.random.normal(k3, (C, C), dtype=jnp.float32) * C ** (-0.5)
        proj_b = jnp.zeros((C,), dtype=jnp.float32)
        return {'x': x, 'qkv_w': qkv_w, 'proj_w': proj_w, 'proj_b': proj_b}
    _L1_attn_all = _L1_attn_setup()
    _L1_attn_in = {k: v for k, v in _L1_attn_all.items() if k in ('qkv_w', 'proj_w', 'proj_b')}
    del _L1_attn_all

    def _L1_ffn_setup():
        import jax, jax.numpy as jnp
        import numpy as np
        E4M3_MAX = 448.0

        def qdq(x, scale, fp8_dtype, fmax):
            scaled = x / scale
            clipped = jnp.clip(scaled, -fmax, fmax)
            return clipped.astype(fp8_dtype).astype(x.dtype) * scale.astype(x.dtype)
        key = jax.random.key(seed)
        k1, k2, k3 = jax.random.split(key, 3)
        B, S, D, F = (8, 2048, 128, 128)
        x = jax.random.normal(k1, (B, S, D), jnp.float32)
        kernel = jax.random.normal(k2, (D, F), jnp.float32) * (1.0 / np.sqrt(D))
        bias = jax.random.normal(k3, (F,), jnp.float32) * 0.01
        return {'x': x, 'kernel': kernel, 'bias': bias, 'input_scale': jnp.ones((1,), jnp.float32), 'kernel_scale': jnp.ones((1,), jnp.float32), 'output_grad_scale': jnp.ones((1,), jnp.float32)}
    _L1_ffn_all = _L1_ffn_setup()
    _L1_ffn_in = {k: v for k, v in _L1_ffn_all.items() if k in ('kernel', 'bias', 'input_scale', 'kernel_scale', 'output_grad_scale')}
    del _L1_ffn_all
    return {'x': x, 'L0_conv_w_phi': _L0_conv_in['w_phi'], 'L0_conv_w_theta': _L0_conv_in['w_theta'], 'L0_conv_w_g': _L0_conv_in['w_g'], 'L0_conv_w_mask': _L0_conv_in['w_mask'], 'L1_attn_qkv_w': _L1_attn_in['qkv_w'], 'L1_attn_proj_w': _L1_attn_in['proj_w'], 'L1_attn_proj_b': _L1_attn_in['proj_b'], 'L1_ffn_kernel': _L1_ffn_in['kernel'], 'L1_ffn_bias': _L1_ffn_in['bias'], 'L1_ffn_input_scale': _L1_ffn_in['input_scale'], 'L1_ffn_kernel_scale': _L1_ffn_in['kernel_scale'], 'L1_ffn_output_grad_scale': _L1_ffn_in['output_grad_scale']}

def reference(x, L0_conv_w_phi, L0_conv_w_theta, L0_conv_w_g, L0_conv_w_mask, L1_attn_qkv_w, L1_attn_proj_w, L1_attn_proj_b, L1_ffn_kernel, L1_ffn_bias, L1_ffn_input_scale, L1_ffn_kernel_scale, L1_ffn_output_grad_scale):
    import jax
    import jax.numpy as jnp

    def _L0_conv_ref(x, w_phi, w_theta, w_g, w_mask):
        import jax, jax.numpy as jnp
        import numpy as np
        CHANNEL = 128
        INTER = CHANNEL // 2
        b, c, h, w = x.shape
        inter = c // 2
        n = h * w // 2
        phi = jnp.einsum('oc,bchw->bohw', w_phi, x).reshape(b, c, n)
        theta = jnp.einsum('oc,bchw->bohw', w_theta, x).reshape(b, c, n)
        theta = jnp.transpose(theta, (0, 2, 1))
        g = jnp.einsum('oc,bchw->bohw', w_g, x).reshape(b, c, n)
        g = jnp.transpose(g, (0, 2, 1))
        attn = jnp.matmul(theta, phi)
        attn = jax.nn.softmax(attn, axis=1)
        y = jnp.matmul(attn, g)
        y = jnp.transpose(y, (0, 2, 1)).reshape(b, inter, h, w)
        mask = jnp.einsum('oc,bchw->bohw', w_mask, y)
        return mask + x

    def _L1_attn_ref(x, qkv_w, proj_w, proj_b):
        import jax, jax.numpy as jnp
        import numpy as np
        NUM_HEADS = 8
        WINDOW_SIZES = (9, 17)
        B, N, C = x.shape
        H = NUM_HEADS
        D = C // H
        qkv = (x @ qkv_w.T).reshape(B, N, 3, H, D)
        q = qkv[:, :, 0].transpose(0, 2, 1, 3)
        k = qkv[:, :, 1].transpose(0, 2, 1, 3)
        v = qkv[:, :, 2].transpose(0, 2, 1, 3)
        scale = D ** (-0.5)
        scores = jnp.einsum('bhnd,bhmd->bhnm', q, k) * scale
        idx = jnp.arange(N)
        dist = jnp.abs(idx[:, None] - idx[None, :])
        max_neg = -jnp.finfo(scores.dtype).max
        out = jnp.zeros_like(q)
        for ws in WINDOW_SIZES:
            mask = dist <= ws // 2
            masked = jnp.where(mask[None, None], scores, max_neg)
            attn = jax.nn.softmax(masked, axis=-1)
            out = out + jnp.einsum('bhnm,bhmd->bhnd', attn, v)
        out = out / len(WINDOW_SIZES)
        out = out.transpose(0, 2, 1, 3).reshape(B, N, C)
        return out @ proj_w.T + proj_b

    def _L1_ffn_ref(x, kernel, bias, input_scale, kernel_scale, output_grad_scale):
        import jax, jax.numpy as jnp
        import numpy as np
        E4M3_MAX = 448.0

        def qdq(x, scale, fp8_dtype, fmax):
            scaled = x / scale
            clipped = jnp.clip(scaled, -fmax, fmax)
            return clipped.astype(fp8_dtype).astype(x.dtype) * scale.astype(x.dtype)
        B, S, D = x.shape
        inp_mat = x.reshape(-1, D)
        inp_q = qdq(inp_mat, input_scale, jnp.float8_e4m3fn, E4M3_MAX)
        ker_q = qdq(kernel, kernel_scale, jnp.float8_e4m3fn, E4M3_MAX)
        out = inp_q @ ker_q
        b = bias.astype(jnp.bfloat16).astype(jnp.float32)
        out = out + b
        return out.reshape(B, S, out.shape[-1])

    def _gn(v, G=32, eps=1e-05):
        B_, C_, H_, W_ = v.shape
        g = v.reshape(B_, G, C_ // G, H_, W_)
        m = jnp.mean(g, axis=(2, 3, 4), keepdims=True)
        s = jnp.var(g, axis=(2, 3, 4), keepdims=True)
        return ((g - m) / jnp.sqrt(s + eps)).reshape(v.shape)

    def _ln_c(v, eps=1e-06):
        m = jnp.mean(v, axis=1, keepdims=True)
        s = jnp.var(v, axis=1, keepdims=True)
        return (v - m) / jnp.sqrt(s + eps)

    def _ln_t(v, eps=1e-05):
        m = jnp.mean(v, axis=-1, keepdims=True)
        s = jnp.var(v, axis=-1, keepdims=True)
        return (v - m) / jnp.sqrt(s + eps)

    def _to_tokens(v):
        B_, C_, H_, W_ = v.shape
        return v.reshape(B_, C_, H_ * W_).transpose(0, 2, 1)

    def _from_tokens(t, like):
        B_, C_, H_, W_ = like.shape
        return t.transpose(0, 2, 1).reshape(B_, C_, H_, W_)
    x = _L0_conv_ref(x, L0_conv_w_phi, L0_conv_w_theta, L0_conv_w_g, L0_conv_w_mask)
    t = _to_tokens(x)
    t = t + _L1_attn_ref(_ln_t(t), L1_attn_qkv_w, L1_attn_proj_w, L1_attn_proj_b)
    t = t + _L1_ffn_ref(_ln_t(t), L1_ffn_kernel, L1_ffn_bias, L1_ffn_input_scale, L1_ffn_kernel_scale, L1_ffn_output_grad_scale)
    x = _from_tokens(t, x)
    return x

_drawn_inputs = setup_inputs


def setup_inputs(seed=0):
    import zlib

    import numpy as np

    out = dict(_drawn_inputs(seed))
    spreads = {'L1_attn_proj_b': (0.0, 0.1)}
    factors = {'L1_ffn_bias': 8.0}
    for name, (base, spread) in spreads.items():
        noise = np.random.default_rng([zlib.crc32(name.encode()), seed]).standard_normal(out[name].shape)
        drawn = base * np.exp(spread * noise) if base else spread * noise
        out[name] = jnp.asarray(drawn.astype(out[name].dtype))
    for name, factor in factors.items():
        out[name] = (out[name] * factor).astype(out[name].dtype)
    return out
```

```python
from contextlib import ExitStack

import concourse.bass as bass
from concourse import mybir


F32 = mybir.dt.float32
BF16 = mybir.dt.bfloat16
FP8 = mybir.dt.float8e4
ALU = mybir.AluOpType
ACT = mybir.ActivationFunctionType
AX = mybir.AxisListType

UNITS = 8
C = 128
HALF = 128
TOK = 2 * HALF
INTER = 64
HEADS = 8
PAIRS = HEADS // 2
D = C // HEADS
RADIUS = (4, 8)
KINDS = len(RADIUS)
QW = C // HEADS
KW = QW + 2 * RADIUS[1]
WINDOWS = TOK // QW
BANKS = 2
WB = WINDOWS // BANKS
PAD = RADIUS[1]
PADDED = PAD + TOK + PAD
SCALE = float(D) ** -0.5
NEG = -1.0e37
LN_EPS = 1e-5
E4M3_MAX = 448.0
TINY = 2.0 ** -5
ACT_HEADS = 3


def hybrid_block_kernel(nc, x, w_phi, w_theta, w_g, w_mask, qkv_w, proj_w, proj_b,
                        ffn_kernel, ffn_bias, input_scale, kernel_scale, out):
    ctx = ExitStack()
    with ctx:
        def sb(name, shape, dt=F32):
            return ctx.enter_context(nc.sbuf_tensor(name, shape, dt))

        def sem(name):
            return ctx.enter_context(nc.semaphore(name))

        phi_w = sb("phi_w", [INTER, C])
        theta_w = sb("theta_w", [INTER, C])
        g_w = sb("g_w", [INTER, C])
        mask_w = sb("mask_w", [C, INTER])
        mask_wt = sb("mask_wt", [INTER, C])
        qkv_rows = sb("qkv_rows", [C, 3, C])
        proj_rows = sb("proj_rows", [C, C])
        bilinear_t = sb("bilinear_t", [C, C])
        gmask_t = sb("gmask_t", [C, C])
        qkv_t = sb("qkv_t", [C, 3, C])
        proj_t = sb("proj_t", [C, C])
        proj_bias = sb("proj_bias", [HALF, C])
        ffn_k = sb("ffn_k", [C, C])
        ffn_kc = sb("ffn_kc", [C, C])
        ffn_ks = sb("ffn_ks", [C, C])
        k_half8 = sb("k_half8", [C, C], FP8)
        k_tiny8 = sb("k_tiny8", [C, C], FP8)
        k_tinyhalf8 = sb("k_tinyhalf8", [C, C], FP8)
        k_part = sb("k_part", [C, 2, C])
        kq = sb("kq", [C, C], BF16)
        kq_twice = sb("kq_twice", [C, C], BF16)
        kq_minus = sb("kq_minus", [C, C], BF16)
        bias_raw = sb("bias_raw", [C, 1])
        bias_bf = sb("bias_bf", [C, 1], BF16)
        bias_col = sb("bias_col", [C, 1])
        scales = sb("scales", [C, 2])
        scale_inv = sb("scale_inv", [C, 2])
        scale_prod = sb("scale_prod", [C, 1])
        identity = sb("identity", [C, C])
        head_mask = sb("head_mask", [C, HEADS])
        pair_mask = sb("pair_mask", [C, PAIRS])
        parity_mask = sb("parity_mask", [C, 2])
        query_sel = sb("query_sel", [QW, HEADS, QW], BF16)
        band_mask = sb("band_mask", [QW, WINDOWS, KINDS, KW], BF16)
        minus_half = sb("minus_half", [HALF, 2])
        ln_eps = sb("ln_eps", [HALF, 2])

        x_all = sb("x_all", [C, UNITS, TOK])
        t_all = sb("t_all", [HALF, UNITS, TOK])
        tb_all = sb("tb_all", [HALF, UNITS, TOK])
        out_all = sb("out_all", [C, UNITS, TOK])

        x_cur = sb("x_cur", [C, TOK])
        u_sb = sb("u_sb", [C, TOK])
        col_nmax = sb("col_nmax", [HALF, 1])
        col_sum = sb("col_sum", [HALF, 1])
        col_inv = sb("col_inv", [HALF, 1])
        e_sb = sb("e_sb", [HALF, HALF])
        g_sb = sb("g_sb", [HALF, TOK])
        st1 = sb("st1", [HALF, 2, 6])
        mv1 = sb("mv1", [HALF, 2, 2])
        ve1 = sb("ve1", [HALF, 2])
        rstd1 = sb("rstd1", [HALF, 2])
        z_sb = sb("z_sb", [HALF, TOK])
        zt_sb = sb("zt_sb", [C, TOK])
        qt_sb = sb("qt_sb", [C, TOK])
        q_bd = sb("q_bd", [C, WINDOWS, HEADS, QW])
        k_pad = sb("k_pad", [C, PADDED])
        v_pad = sb("v_pad", [C, PADDED])
        v_win = sb("v_win", [C, WINDOWS, 32])
        v_bd = sb("v_bd", [C, WINDOWS, C])
        row_max = sb("row_max", [C, BANKS, WB, KINDS])
        row_sum = sb("row_sum", [C, BANKS, WB, KINDS])
        row_inv = sb("row_inv", [C, BANKS, WB, KINDS])
        diff = sb("diff", [C, BANKS, WB, KINDS, KW])
        expd = sb("expd", [C, BANKS, WB, KINDS, KW])
        prob2 = sb("prob2", [C, BANKS, WB, KINDS, KW])
        prob = sb("prob", [C, BANKS, WB, KW])
        prob_t = sb("prob_t", [C, BANKS, WB, 32])
        att_even = sb("att_even", [C, WINDOWS, QW])
        att_t = sb("att_t", [C, WINDOWS, QW])
        t2_sb = sb("t2_sb", [HALF, TOK])
        st2 = sb("st2", [HALF, 2, 6])
        mv2 = sb("mv2", [HALF, 2, 2])
        ve2 = sb("ve2", [HALF, 2])
        rstd2 = sb("rstd2", [HALF, 2])
        z2_sb = sb("z2_sb", [HALF, TOK])
        t2b = sb("t2b", [C, TOK])
        y_sb = sb("y_sb", [C, TOK])
        y_tiny = sb("y_tiny", [C, TOK])
        y_half8 = sb("y_half8", [C, TOK], FP8)
        y_tiny8 = sb("y_tiny8", [C, TOK], FP8)
        y_tinyhalf8 = sb("y_tinyhalf8", [C, TOK], FP8)

        bank = [ctx.enter_context(nc.psum_tensor(f"bank{i}", [128, 512], F32)) for i in range(8)]
        ps_u, ps_attn, ps_zt = bank[0][:, 0:TOK], bank[0][:, 0:HALF], bank[0][:, 0:TOK]
        ps_g, ps_t = bank[1][:, 0:TOK], bank[1][:, 0:TOK]
        ps_q, ps_k = bank[2][:, 0:TOK], bank[2][:, TOK:2 * TOK]
        ps_v = bank[3][:, 0:TOK]
        ps_scores = [bank[4 + g][:, :] for g in range(BANKS)]
        ps_pv, ps_z2t, ps_t2t = bank[6][:, :], bank[6][:, 0:TOK], bank[6][:, TOK:2 * TOK]
        ps_proj, ps_ffn = bank[7][:, 0:TOK], bank[7][:, 0:TOK]

        x_first, x_rest = sem("x_first"), sem("x_rest")
        bilinear_in, gmask_in, qkv_in, proj_in = sem("bilinear_in"), sem("gmask_in"), sem("qkv_in"), sem("proj_in")
        ffn_in = sem("ffn_in")
        pool_const = sem("pool_const")
        identity_made, masks_made, heads_made, zeros_made = (
            sem("identity_made"), sem("masks_made"), sem("heads_made"), sem("zeros_made"))
        weight_mm, weight_done = sem("weight_mm"), sem("weight_done")
        quant_step, parity_made, kernel_done = sem("quant_step"), sem("parity_made"), sem("kernel_done")

        x_ready = sem("x_ready")
        u_mm, u_done = sem("u_mm"), sem("u_done")
        attn_mm, g_mm = sem("attn_mm"), sem("g_mm")
        nmax_done, e_done, inv_done, g_done = sem("nmax_done"), sem("e_done"), sem("inv_done"), sem("g_done")
        t_mm, t_kept = sem("t_mm"), sem("t_kept")
        stats1, aggr1, var1, rstd1_done = sem("stats1"), sem("aggr1"), sem("var1"), sem("rstd1_done")
        z_done, zt_mm, zt_done = sem("z_done"), sem("zt_mm"), sem("zt_done")
        qkv_mm, k_done, v_done, q_done = sem("qkv_mm"), sem("k_done"), sem("v_done"), sem("q_done")
        qbd_act, qbd_dve, vwin_done, vbd_done = sem("qbd_act"), sem("qbd_dve"), sem("vwin_done"), sem("vbd_done")
        tb_done = sem("tb_done")
        scores_mm = [sem(f"scores_mm{g}") for g in range(BANKS)]
        max_done = [sem(f"max_done{g}") for g in range(BANKS)]
        diff_done = [sem(f"diff_done{g}") for g in range(BANKS)]
        exp_done = [sem(f"exp_done{g}") for g in range(BANKS)]
        sum_done = [sem(f"sum_done{g}") for g in range(BANKS)]
        rinv_done = [sem(f"rinv_done{g}") for g in range(BANKS)]
        scaled = [sem(f"scaled{g}") for g in range(BANKS)]
        prob_done = [sem(f"prob_done{g}") for g in range(BANKS)]
        probt_done = [sem(f"probt_done{g}") for g in range(BANKS)]
        pv_mm, even_done, att_done = sem("pv_mm"), sem("even_done"), sem("att_done")
        proj_mm, t2_done = sem("proj_mm"), sem("t2_done")
        stats2, aggr2, var2, rstd2_done = sem("stats2"), sem("aggr2"), sem("var2"), sem("rstd2_done")
        z2_done, z2t_mm, t2b_done = sem("z2_done"), sem("z2t_mm"), sem("t2b_done")
        y_done, yhalf_done, ytiny_done = sem("y_done"), sem("yhalf_done"), sem("ytiny_done")
        tiny8_done, ffn_mm, out_done, out_sent = sem("tiny8_done"), sem("ffn_mm"), sem("out_done"), sem("out_sent")

        def wait(engine, s, units):
            if not (isinstance(units, int) and units <= 0):
                engine.wait_ge(s, units)

        def part(engine):
            engine.wait_ge(zeros_made, 1)

        def pipeline(engine, step):
            for k in range(3):
                step(k, True, k >= 1, k >= 2)
            with engine.Fori(3, UNITS - 1) as k:
                step(k, True, True, True)
            step(UNITS - 1, True, True, True)
            step(UNITS, False, True, True)
            step(UNITS + 1, False, False, True)

        block = ctx.enter_context(nc.Block())

        @block.sync
        def _(sp):
            sp.dma_start(x_cur[:, :], x[0]).then_inc(x_first, 16)
            sp.dma_start(g_w[:, :], w_g).then_inc(gmask_in, 16)
            sp.dma_start(mask_w[:, :], w_mask).then_inc(gmask_in, 16)
            sp.dma_start(qkv_rows[:, :, :], qkv_w.rearrange("(t o) c -> o t c", t=3)).then_inc(qkv_in, 16)
            sp.dma_start(x_all[:, 1:UNITS, :], x[1:UNITS].rearrange("u c t -> c u t")).then_inc(x_rest, 16)
            with sp.Fori(0, UNITS) as u:
                sp.wait_ge(out_done, u + 1)
                sp.dma_start(out[u], out_all[:, u, :]).then_inc(out_sent, 16)
            sp.wait_ge(out_sent, 16 * UNITS)

        @block.tensor
        def _(pe):
            mm = nc.tensor.matmul

            pe.wait_ge(bilinear_in, 32)
            mm(bank[0][:, 0:C], theta_w[:, :], phi_w[:, :], start=True, stop=True).then_inc(weight_mm, 1)
            pe.wait_ge(identity_made, 1)
            pe.wait_ge(gmask_in, 32)
            nc.tensor.transpose(bank[1][0:INTER, 0:C], mask_w[:, :], identity[:, :]).then_inc(weight_mm, 1)
            pe.wait_ge(qkv_in, 16)
            for i in range(3):
                nc.tensor.transpose(bank[3][:, i * C:(i + 1) * C], qkv_rows[:, i, :], identity[:, :]).then_inc(weight_mm, 1)
            pe.wait_ge(proj_in, 32)
            nc.tensor.transpose(bank[3][:, 3 * C:4 * C], proj_rows[:, :], identity[:, :]).then_inc(weight_mm, 1)
            pe.wait_ge(weight_done, 2)
            mm(bank[2][:, 0:C], g_w[:, :], mask_wt[:, :], start=True, stop=True).then_inc(weight_mm, 1)
            pe.wait_ge(weight_done, 5)
            pe.wait_ge(masks_made, 1)
            pe.wait_ge(zeros_made, 1)

            def halves(s):
                return slice(s * HALF, (s + 1) * HALF)

            def apply_bilinear(u):
                wait(pe, x_ready, u)
                if isinstance(u, int) and u == 0:
                    pe.wait_ge(x_first, 16)
                mm(ps_u, bilinear_t[:, :], x_cur[:, :], start=True, stop=True).then_inc(u_mm, 1)

            def attention_and_g(u):
                wait(pe, u_done, u + 1)
                for s in range(2):
                    last = mm(ps_attn, x_cur[:, halves(s)], u_sb[:, halves(s)], start=(s == 0), stop=(s == 1))
                last.then_inc(attn_mm, 1)
                for s in range(2):
                    last = mm(ps_g[:, halves(s)], x_cur[:, halves(s)], gmask_t[:, :], start=True, stop=True)
                last.then_inc(g_mm, 1)

            def mix_tokens(u):
                wait(pe, e_done, u + 1)
                wait(pe, g_done, u + 1)
                mm(ps_t, e_sb[:, :], g_sb[:, :], start=True, stop=False)
                for s in range(2):
                    last = mm(ps_t[:, halves(s)], x_cur[:, halves(s)], identity[:, :], start=False, stop=(s == 1))
                last.then_inc(t_mm, 1)

            def turn_z(u):
                wait(pe, z_done, u + 1)
                for s in range(2):
                    last = nc.tensor.transpose(ps_zt[:, halves(s)], z_sb[:, halves(s)], identity[:, :])
                last.then_inc(zt_mm, 1)

            def project_qkv(u):
                wait(pe, zt_done, u + 1)
                wait(pe, v_done, u)
                for i, o in ((1, ps_k), (2, ps_v), (0, ps_q)):
                    last = mm(o, qkv_t[:, i, :], zt_sb[:, :], start=True, stop=True)
                last.then_inc(qkv_mm, 1)

            def scores(u, g):
                if g == 0:
                    wait(pe, qbd_act, u + 1)
                    wait(pe, qbd_dve, u + 1)
                    wait(pe, k_done, u + 1)
                wait(pe, diff_done[g], u)
                mm(ps_scores[g], query_sel[:, :, :].rearrange("p h q -> p (h q)"),
                   band_mask[:, g * WB:(g + 1) * WB, :, :].rearrange("p w k n -> p (w k n)"),
                   start=True, stop=False)
                for w in range(g * WB, (g + 1) * WB):
                    o = ps_scores[g].rearrange("p (w n) -> p w n", w=WB)[:, w - g * WB, :]
                    keys = k_pad[:, w * QW:w * QW + KW].unsqueeze(1).to_broadcast([C, KINDS, KW])
                    last = mm(o, q_bd[:, w, :, :].rearrange("p h q -> p (h q)"), keys,
                              start=False, stop=(w == (g + 1) * WB - 1))
                last.then_inc(scores_mm[g], 1)

            def weigh_values(u):
                wait(pe, vbd_done, u + 1)
                for g in range(BANKS):
                    wait(pe, probt_done[g], u + 1)
                    for w in range(WB):
                        at = g * WB + w
                        last = mm(ps_pv[:, at * 32:(at + 1) * 32], v_bd[:, at, :], prob_t[:, g, w, :],
                                  start=True, stop=True)
                last.then_inc(pv_mm, 1)

            def project(u):
                wait(pe, att_done, u + 1)
                a = att_t[:, :, :].rearrange("p w q -> p (w q)")
                for s in range(2):
                    last = mm(ps_proj[:, halves(s)], a[:, halves(s)], proj_t[:, :], start=True, stop=True)
                last.then_inc(proj_mm, 1)

            def turn_back(u):
                wait(pe, z2_done, u + 1)
                for s in range(2):
                    nc.tensor.transpose(ps_z2t[:, halves(s)], z2_sb[:, halves(s)], identity[:, :])
                for s in range(2):
                    last = nc.tensor.transpose(ps_t2t[:, halves(s)], t2_sb[:, halves(s)], identity[:, :])
                last.then_inc(z2t_mm, 1)

            def feed_forward(u):
                part(pe)
                if isinstance(u, int) and u == 0:
                    pe.wait_ge(kernel_done, 3)
                wait(pe, yhalf_done, u + 1)
                wait(pe, tiny8_done, u + 1)
                mm(ps_ffn, kq_twice[:, :], y_half8[:, :], start=True, stop=False)
                mm(ps_ffn, kq[:, :], y_tiny8[:, :], start=False, stop=False)
                mm(ps_ffn, kq_minus[:, :], y_tinyhalf8[:, :], start=False, stop=True).then_inc(ffn_mm, 1)

            def step(k, a, b, c):
                if a:
                    apply_bilinear(k)
                if b:
                    scores(k - 1, 0)
                if a:
                    attention_and_g(k)
                if b:
                    scores(k - 1, 1)
                if c:
                    weigh_values(k - 2)
                if a:
                    mix_tokens(k)
                if c:
                    project(k - 2)
                if a:
                    turn_z(k)
                if c:
                    turn_back(k - 2)
                if a:
                    project_qkv(k)
                if c:
                    feed_forward(k - 2)

            pipeline(pe, step)

        @block.scalar
        def _(act):
            act.dma_start(theta_w[:, :], w_theta).then_inc(bilinear_in, 16)
            act.dma_start(phi_w[:, :], w_phi).then_inc(bilinear_in, 16)
            act.dma_start(proj_rows[:, :], proj_w).then_inc(proj_in, 16)
            act.dma_start(proj_bias[:, :], proj_b.unsqueeze(0).to_broadcast([HALF, C])).then_inc(proj_in, 16)
            act.dma_start(ffn_k[:, :], ffn_kernel).then_inc(ffn_in, 16)
            act.dma_start(bias_raw[:, :], ffn_bias.unsqueeze(1)).then_inc(ffn_in, 16)
            act.dma_start(scales[:, 0:1], input_scale.unsqueeze(0).to_broadcast([C, 1])).then_inc(ffn_in, 16)
            act.dma_start(scales[:, 1:2], kernel_scale.unsqueeze(0).to_broadcast([C, 1])).then_inc(ffn_in, 16)
            nc.scalar.preload_act_table(ACT.Exp)

            act.wait_ge(weight_mm, 1)
            nc.scalar.copy(bilinear_t[:, :], bank[0][:, 0:C]).then_inc(weight_done, 1)
            act.wait_ge(weight_mm, 2)
            nc.scalar.copy(mask_wt[:, :], bank[1][0:INTER, 0:C]).then_inc(weight_done, 1)
            act.wait_ge(weight_mm, 6)
            nc.scalar.copy(qkv_t[:, :, :].rearrange("p t c -> p (t c)"), bank[3][:, 0:3 * C]).then_inc(weight_done, 1)
            nc.scalar.copy(proj_t[:, :], bank[3][:, 3 * C:4 * C]).then_inc(weight_done, 1)
            act.wait_ge(weight_mm, 7)
            nc.scalar.copy(gmask_t[:, :], bank[2][:, 0:C]).then_inc(weight_done, 1)
            act.wait_ge(heads_made, 1)
            act.wait_ge(parity_made, 1)

            def copy_u(u):
                wait(act, u_mm, u + 1)
                wait(act, attn_mm, u)
                nc.scalar.copy(u_sb[:, :], ps_u).then_inc(u_done, 1)

            def column_exp(u):
                wait(act, nmax_done, u + 1)
                wait(act, t_mm, u)
                nc.scalar.activation(e_sb[:, :], ps_attn, ACT.Exp, bias=col_nmax[:, 0:1], scale=1.0,
                                     accum_out=col_sum[:, 0:1]).then_inc(e_done, 1)

            def scale_g(u):
                wait(act, g_mm, u + 1)
                wait(act, inv_done, u + 1)
                nc.scalar.activation(g_sb[:, :], ps_g, ACT.Copy, scale=col_inv[:, 0:1]).then_inc(g_done, 1)

            def keep_t(u):
                wait(act, t_mm, u + 1)
                nc.scalar.copy(t_all[:, u, :], ps_t).then_inc(t_kept, 1)

            def copy_zt(u):
                wait(act, zt_mm, u + 1)
                nc.scalar.copy(zt_sb[:, :], ps_zt).then_inc(zt_done, 1)

            def copy_qkv(u):
                wait(act, qkv_mm, u + 1)
                wait(act, scores_mm[1], u)
                nc.scalar.copy(k_pad[:, PAD:PAD + TOK], ps_k).then_inc(k_done, 1)
                wait(act, qbd_dve, u)
                nc.scalar.copy(qt_sb[:, :], ps_q).then_inc(q_done, 1)
                for h in range(ACT_HEADS):
                    last = nc.scalar.activation(q_bd[:, :, h, :], ps_q.rearrange("p (w q) -> p w q", q=QW),
                                                ACT.Copy, scale=head_mask[:, h:h + 1])
                last.then_inc(qbd_act, 1)
                wait(act, vwin_done, u)
                nc.scalar.mul(v_pad[:, PAD:PAD + TOK], ps_v, 1.0 / KINDS).then_inc(v_done, 1)

            def band_exp(u, g):
                wait(act, diff_done[g], u + 1)
                wait(act, scaled[g], u)
                wait(act, sum_done[g], u)
                nc.scalar.activation(expd[:, g].rearrange("p w k n -> p (w k n)"),
                                     diff[:, g].rearrange("p w k n -> p (w k n)"),
                                     ACT.Exp, scale=SCALE).then_inc(exp_done[g], 1)

            def pick_even(u):
                wait(act, pv_mm, u + 1)
                wait(act, att_done, u)
                nc.scalar.activation(att_even[:, :, :],
                                     ps_pv.rearrange("p (w e q) -> p w e q", e=2, q=QW)[:, :, 0, :],
                                     ACT.Copy, scale=parity_mask[:, 0:1]).then_inc(even_done, 1)

            def add_bias(u):
                if isinstance(u, int) and u == 0:
                    act.wait_ge(quant_step, 2)
                wait(act, z2t_mm, u + 1)
                wait(act, y_done, u + 1)
                wait(act, out_done, u)
                nc.scalar.activation(t2b[:, :], ps_t2t, ACT.Identity, bias=bias_col[:, 0:1],
                                     scale=1.0).then_inc(t2b_done, 1)

            def tiny_to_fp8(u):
                part(act)
                wait(act, ytiny_done, u + 1)
                wait(act, ffn_mm, u)
                nc.scalar.activation(y_tiny8[:, :], y_tiny[:, :], ACT.Copy, saturate=False)
                nc.scalar.activation(y_tinyhalf8[:, :], y_tiny[:, :], ACT.Copy, scale=0.5,
                                     saturate=False).then_inc(tiny8_done, 1)

            def step(k, a, b, c):
                if a:
                    copy_u(k)
                if b:
                    band_exp(k - 1, 0)
                if a:
                    column_exp(k)
                    scale_g(k)
                if b:
                    band_exp(k - 1, 1)
                if c:
                    pick_even(k - 2)
                if a:
                    keep_t(k)
                    copy_zt(k)
                if c:
                    add_bias(k - 2)
                    tiny_to_fp8(k - 2)
                if a:
                    copy_qkv(k)

            pipeline(act, step)

        @block.vector
        def _(dve):
            v = nc.vector

            dve.wait_ge(heads_made, 1)
            v.tensor_reduce(parity_mask[:, :], head_mask[:, :].rearrange("p (i e) -> p e i", e=2),
                            AX.X, ALU.add).then_inc(parity_made, 1)

            def quantise_kernel():
                dve.wait_ge(ffn_in, 64)
                v.tensor_copy(bias_bf[:, :], bias_raw[:, :]).then_inc(quant_step, 1)
                dve.wait_ge(quant_step, 1)
                v.tensor_copy(bias_col[:, :], bias_bf[:, :]).then_inc(quant_step, 1)
                v.reciprocal(scale_inv[:, :], scales[:, :]).then_inc(quant_step, 1)
                v.tensor_tensor(scale_prod[:, :], scales[:, 0:1], scales[:, 1:2], ALU.mult).then_inc(quant_step, 1)
                dve.wait_ge(quant_step, 4)
                v.tensor_scalar(ffn_ks[:, :], ffn_k[:, :], scale_inv[:, 1:2], E4M3_MAX, ALU.mult, ALU.min).then_inc(quant_step, 1)
                dve.wait_ge(quant_step, 5)
                v.tensor_scalar(k_half8[:, :], ffn_ks[:, :], -E4M3_MAX, 0.5, ALU.max, ALU.mult, saturate=False).then_inc(quant_step, 1)
                v.tensor_scalar(ffn_kc[:, :], ffn_ks[:, :], TINY, -TINY, ALU.min, ALU.max).then_inc(quant_step, 1)
                dve.wait_ge(quant_step, 7)
                v.tensor_scalar(k_tiny8[:, :], ffn_kc[:, :], 1.0, None, ALU.mult, saturate=False).then_inc(quant_step, 1)
                v.tensor_scalar(k_tinyhalf8[:, :], ffn_kc[:, :], 0.5, None, ALU.mult, saturate=False).then_inc(quant_step, 1)
                dve.wait_ge(quant_step, 9)
                v.scalar_tensor_tensor(k_part[:, 0, :], k_tinyhalf8[:, :], -2.0, k_tiny8[:, :],
                                       ALU.mult, ALU.add).then_inc(quant_step, 1)
                dve.wait_ge(quant_step, 10)
                v.scalar_tensor_tensor(k_part[:, 1, :], k_half8[:, :], 2.0, k_part[:, 0, :],
                                       ALU.mult, ALU.add).then_inc(quant_step, 1)
                dve.wait_ge(quant_step, 11)
                v.tensor_copy(kq[:, :], k_part[:, 1, :]).then_inc(kernel_done, 1)
                v.tensor_scalar(kq_twice[:, :], k_part[:, 1, :], 2.0, None, ALU.mult).then_inc(kernel_done, 1)
                v.tensor_scalar(kq_minus[:, :], k_part[:, 1, :], -2.0, None, ALU.mult).then_inc(kernel_done, 1)

            def halves(s):
                return slice(s * HALF, (s + 1) * HALF)

            def column_max(u):
                wait(dve, attn_mm, u + 1)
                v.tensor_reduce(col_nmax[:, :], ps_attn, AX.X, ALU.max, negate=True).then_inc(nmax_done, 1)

            def column_inverse(u):
                wait(dve, e_done, u + 1)
                wait(dve, g_done, u)
                v.reciprocal(col_inv[:, :], col_sum[:, :]).then_inc(inv_done, 1)

            def stats_first(u):
                wait(dve, t_kept, u + 1)
                v.bn_stats(st1[:, 0, :], t_all[:, u, halves(0)])
                v.bn_stats(st1[:, 1, :], t_all[:, u, halves(1)]).then_inc(stats1, 1)
                part(dve)
                wait(dve, stats1, u + 1)
                v.bn_aggr(mv1[:, 0, :], st1[:, 0, :])
                v.bn_aggr(mv1[:, 1, :], st1[:, 1, :]).then_inc(aggr1, 1)

            def norm_first(u):
                wait(dve, rstd1_done, u + 1)
                wait(dve, zt_mm, u)
                for s in range(2):
                    last = v.tensor_scalar(z_sb[:, halves(s)], t_all[:, u, halves(s)], mv1[:, s, 0:1],
                                           rstd1[:, s:s + 1], ALU.subtract, ALU.mult)
                last.then_inc(z_done, 1)

            def spread_heads(u):
                wait(dve, q_done, u + 1)
                wait(dve, scores_mm[1], u)
                for h in range(ACT_HEADS, HEADS):
                    last = v.tensor_scalar(q_bd[:, :, h, :], qt_sb[:, :].rearrange("p (w q) -> p w q", q=QW),
                                           head_mask[:, h:h + 1], None, ALU.mult)
                last.then_inc(qbd_dve, 1)

            def window_values(u):
                wait(dve, v_done, u + 1)
                wait(dve, vbd_done, u)
                windows = bass.AP(v_pad, 0, [[PADDED, C], [QW, WINDOWS], [1, KW]])
                v.transpose(v_win[:, :, :], windows).then_inc(vwin_done, 1)

            def subtract_max(u, g):
                wait(dve, scores_mm[g], u + 1)
                s = ps_scores[g].rearrange("p (w k n) -> p w k n", w=WB, k=KINDS)
                v.tensor_reduce(row_max[:, g], s, AX.X, ALU.max).then_inc(max_done[g], 1)
                wait(dve, max_done[g], u + 1)
                wait(dve, exp_done[g], u)
                v.tensor_tensor(diff[:, g], s, row_max[:, g].unsqueeze(3).to_broadcast([C, WB, KINDS, KW]),
                                ALU.subtract).then_inc(diff_done[g], 1)

            def row_sums(u, g):
                wait(dve, exp_done[g], u + 1)
                v.tensor_reduce(row_sum[:, g], expd[:, g], AX.X, ALU.add).then_inc(sum_done[g], 1)
                wait(dve, sum_done[g], u + 1)
                wait(dve, scaled[g], u)
                v.reciprocal(row_inv[:, g], row_sum[:, g]).then_inc(rinv_done[g], 1)

            def turn_probs(u, g):
                wait(dve, prob_done[g], u + 1)
                wait(dve, pv_mm, u)
                v.transpose(prob_t[:, g].rearrange("p w n -> p (w n)"),
                            prob[:, g].rearrange("p w n -> p (w n)")).then_inc(probt_done[g], 1)

            def pick_odd(u):
                wait(dve, even_done, u + 1)
                wait(dve, proj_mm, u)
                v.scalar_tensor_tensor(att_t[:, :, :], ps_pv.rearrange("p (w e q) -> p w e q", e=2, q=QW)[:, :, 1, :],
                                       parity_mask[:, 1:2], att_even[:, :, :], ALU.mult, ALU.add).then_inc(att_done, 1)

            def residual(u):
                wait(dve, proj_mm, u + 1)
                wait(dve, tb_done, u + 1)
                wait(dve, z2t_mm, u)
                v.tensor_tensor(t2_sb[:, :], ps_proj, tb_all[:, u, :], ALU.add).then_inc(t2_done, 1)

            def stats_second(u):
                wait(dve, t2_done, u + 1)
                v.bn_stats(st2[:, 0, :], t2_sb[:, halves(0)])
                v.bn_stats(st2[:, 1, :], t2_sb[:, halves(1)]).then_inc(stats2, 1)
                part(dve)
                wait(dve, stats2, u + 1)
                v.bn_aggr(mv2[:, 0, :], st2[:, 0, :])
                v.bn_aggr(mv2[:, 1, :], st2[:, 1, :]).then_inc(aggr2, 1)

            def norm_second(u):
                wait(dve, rstd2_done, u + 1)
                for s in range(2):
                    last = v.tensor_scalar(z2_sb[:, halves(s)], t2_sb[:, halves(s)], mv2[:, s, 0:1],
                                           rstd2[:, s:s + 1], ALU.subtract, ALU.mult)
                last.then_inc(z2_done, 1)

            def quantise(u):
                wait(dve, z2t_mm, u + 1)
                wait(dve, tiny8_done, u)
                wait(dve, ffn_mm, u)
                v.tensor_scalar(y_sb[:, :], ps_z2t, scale_inv[:, 0:1], E4M3_MAX, ALU.mult, ALU.min).then_inc(y_done, 1)
                wait(dve, y_done, u + 1)
                v.tensor_scalar(y_tiny[:, :], y_sb[:, :], TINY, -TINY, ALU.min, ALU.max).then_inc(ytiny_done, 1)
                v.tensor_scalar(y_half8[:, :], y_sb[:, :], -E4M3_MAX, 0.5, ALU.max, ALU.mult,
                                saturate=False).then_inc(yhalf_done, 1)

            def result(u):
                wait(dve, ffn_mm, u + 1)
                wait(dve, t2b_done, u + 1)
                v.scalar_tensor_tensor(out_all[:, u, :], ps_ffn, scale_prod[:, 0:1], t2b[:, :],
                                       ALU.mult, ALU.add).then_inc(out_done, 1)

            def step(k, a, b, c):
                if b:
                    subtract_max(k - 1, 0)
                if a:
                    column_max(k)
                    column_inverse(k)
                if b:
                    subtract_max(k - 1, 1)
                    row_sums(k - 1, 0)
                if c:
                    pick_odd(k - 2)
                if a:
                    stats_first(k)
                if b:
                    row_sums(k - 1, 1)
                if c:
                    residual(k - 2)
                    stats_second(k - 2)
                if a:
                    norm_first(k)
                if b:
                    turn_probs(k - 1, 0)
                if c:
                    norm_second(k - 2)
                    quantise(k - 2)
                if a:
                    spread_heads(k)
                    window_values(k)
                if b:
                    turn_probs(k - 1, 1)
                if c:
                    result(k - 2)
                if isinstance(k, int) and k == 0:
                    quantise_kernel()

            pipeline(dve, step)

        @block.gpsimd
        def _(pool):
            p = nc.gpsimd
            p.memset(identity[:, :], 0.0).then_inc(pool_const, 1)
            pool.wait_ge(pool_const, 1)
            p.affine_select(out=identity[:, :], in_=identity[:, :], compare_op=ALU.not_equal, fill=1.0, base=0,
                            pattern=[[-1, C]], channel_multiplier=1).then_inc(identity_made, 1)
            p.memset(head_mask[:, :], 1.0).then_inc(pool_const, 1)
            pool.wait_ge(pool_const, 2)
            p.affine_select(out=head_mask[:, :], in_=head_mask[:, :], compare_op=ALU.is_ge, fill=0.0, base=0,
                            pattern=[[-D, HEADS]], channel_multiplier=1).then_inc(pool_const, 1)
            pool.wait_ge(pool_const, 3)
            p.affine_select(out=head_mask[:, :], in_=head_mask[:, :], compare_op=ALU.is_ge, fill=0.0, base=D - 1,
                            pattern=[[D, HEADS]], channel_multiplier=-1).then_inc(heads_made, 1)
            p.memset(query_sel[:, :, :], 0.0).then_inc(pool_const, 1)
            pool.wait_ge(pool_const, 4)
            p.affine_select(out=query_sel[:, :, :], in_=query_sel[:, :, :], compare_op=ALU.not_equal, fill=1.0, base=0,
                            pattern=[[0, HEADS], [-1, QW]], channel_multiplier=1).then_inc(pool_const, 1)
            p.memset(band_mask[:, :, :, :], 0.0).then_inc(pool_const, 1)
            pool.wait_ge(pool_const, 6)
            steps = 6
            for kind, r in enumerate(RADIUS):
                for sign in (1, -1):
                    m = band_mask[:, :, kind, :]
                    p.affine_select(out=m, in_=m, compare_op=ALU.is_ge, fill=NEG, base=r - sign * PAD,
                                    pattern=[[0, WINDOWS], [sign, KW]], channel_multiplier=-sign).then_inc(pool_const, 1)
                    steps += 1
                    pool.wait_ge(pool_const, steps)
            m = band_mask[:, 0, :, 0:PAD]
            p.memset(m, NEG)
            m = band_mask[:, WINDOWS - 1, :, KW - PAD:KW]
            p.memset(m, NEG).then_inc(masks_made, 1)
            p.memset(k_pad[:, 0:PAD], 0.0)
            p.memset(k_pad[:, PAD + TOK:PADDED], 0.0)
            p.memset(v_pad[:, 0:PAD], 0.0)
            p.memset(v_pad[:, PAD + TOK:PADDED], 0.0).then_inc(zeros_made, 1)
            p.memset(minus_half[:, :], -0.5)
            p.memset(ln_eps[:, :], LN_EPS)
            p.memset(pair_mask[:, :], 1.0).then_inc(pool_const, 1)
            for sign, base in ((1, 0), (-1, C // PAIRS - 1)):
                steps += 1
                pool.wait_ge(pool_const, steps)
                p.affine_select(out=pair_mask[:, :], in_=pair_mask[:, :], compare_op=ALU.is_ge, fill=0.0, base=base,
                                pattern=[[-sign * (C // PAIRS), PAIRS]], channel_multiplier=sign).then_inc(pool_const, 1)
            pool.wait_ge(pool_const, steps + 1)

            def fetch_x(u):
                part(pool)
                wait(pool, t_mm, u)
                p.tensor_copy(x_cur[:, :], x_all[:, u, :]).then_inc(x_ready, 1)

            def rstd_first(u):
                wait(pool, aggr1, u + 1)
                p.tensor_tensor(ve1[:, :], mv1[:, :, 1], ln_eps[:, :], ALU.add).then_inc(var1, 1)
                wait(pool, var1, u + 1)
                p.tensor_tensor(rstd1[:, :], ve1[:, :], minus_half[:, :], ALU.pow).then_inc(rstd1_done, 1)

            def rstd_second(u):
                wait(pool, aggr2, u + 1)
                p.tensor_tensor(ve2[:, :], mv2[:, :, 1], ln_eps[:, :], ALU.add).then_inc(var2, 1)
                wait(pool, var2, u + 1)
                p.tensor_tensor(rstd2[:, :], ve2[:, :], minus_half[:, :], ALU.pow).then_inc(rstd2_done, 1)

            def add_proj_bias(u):
                wait(pool, t_kept, u + 1)
                b = proj_bias[:, :].unsqueeze(1).to_broadcast([HALF, 2, C])
                p.tensor_tensor(tb_all[:, u, :].rearrange("p (s c) -> p s c", s=2),
                                t_all[:, u, :].rearrange("p (s c) -> p s c", s=2), b, ALU.add).then_inc(tb_done, 1)

            def spread_values(u):
                part(pool)
                wait(pool, vwin_done, u + 1)
                wait(pool, pv_mm, u)
                for i in range(PAIRS):
                    last = p.tensor_scalar(v_bd[:, :, 32 * i:32 * (i + 1)], v_win[:, :, :], pair_mask[:, i:i + 1],
                                           None, ALU.mult)
                last.then_inc(vbd_done, 1)

            def scale_probs(u, g):
                wait(pool, rinv_done[g], u + 1)
                p.tensor_tensor(prob2[:, g], expd[:, g],
                                row_inv[:, g].unsqueeze(3).to_broadcast([C, WB, KINDS, KW]), ALU.mult).then_inc(scaled[g], 1)
                wait(pool, scaled[g], u + 1)
                wait(pool, probt_done[g], u)
                p.tensor_tensor(prob[:, g], prob2[:, g, :, 0, :], prob2[:, g, :, 1, :], ALU.add).then_inc(prob_done[g], 1)

            def step(k, a, b, c):
                if b:
                    add_proj_bias(k - 1)
                    scale_probs(k - 1, 0)
                if a:
                    rstd_first(k)
                    if not isinstance(k, int) or k + 1 < UNITS:
                        if isinstance(k, int) and k == 0:
                            pool.wait_ge(x_rest, 16)
                        fetch_x(k + 1)
                if b:
                    scale_probs(k - 1, 1)
                if c:
                    rstd_second(k - 2)
                if b:
                    spread_values(k - 1)

            pool.wait_ge(proj_in, 32)
            pipeline(pool, step)


_INS = ['x', 'L0_conv_w_phi', 'L0_conv_w_theta', 'L0_conv_w_g', 'L0_conv_w_mask', 'L1_attn_qkv_w',
        'L1_attn_proj_w', 'L1_attn_proj_b', 'L1_ffn_kernel', 'L1_ffn_bias', 'L1_ffn_input_scale',
        'L1_ffn_kernel_scale']


def kernel(**inputs):
    import numpy as _np
    import concourse.bacc as _bacc
    from concourse import mybir as _mybir
    from concourse.bass_utils import run_bass_kernel_spmd as _run

    nc = _bacc.Bacc("TRN2", target_bir_lowering=False, num_devices=1)
    arrays, args = {}, []
    for name in _INS:
        a = _np.ascontiguousarray(inputs[name])
        shape = a.shape
        if name == 'x':
            a = a.reshape(UNITS, C, TOK)
        arrays[f"in_{name}_dram"] = a
        args.append(nc.dram_tensor(f"in_{name}_dram", a.shape, _mybir.dt.from_np(a.dtype), kind="ExternalInput").ap())
    args.append(nc.dram_tensor("out_0_dram", (UNITS, C, TOK), _mybir.dt.float32, kind="ExternalOutput").ap())
    hybrid_block_kernel(nc, *args)
    r = _run(nc, [arrays], core_ids=[0])
    return _np.asarray(r.results[0]["out_0_dram"]).reshape(UNITS, C, 16, 16)
```

```python
from contextlib import ExitStack

import concourse.bass as bass
from concourse import mybir


F32 = mybir.dt.float32
BF16 = mybir.dt.bfloat16
FP8 = mybir.dt.float8e4
ALU = mybir.AluOpType
ACT = mybir.ActivationFunctionType
AX = mybir.AxisListType

UNITS = 8
C = 128
HALF = 128
TOK = 2 * HALF
INTER = 64
HEADS = 8
PAIRS = HEADS // 2
D = C // HEADS
RADIUS = (4, 8)
KINDS = len(RADIUS)
QW = C // HEADS
KW = QW + 2 * RADIUS[1]
WINDOWS = TOK // QW
BANKS = 2
WB = WINDOWS // BANKS
PAD = RADIUS[1]
PADDED = PAD + TOK + PAD
SCALE = float(D) ** -0.5
NEG = -1.0e37
LN_EPS = 1e-5
E4M3_MAX = 448.0
TINY = 2.0 ** -5
QUAD = 2 * D


def hybrid_block_kernel(nc, x, w_phi, w_theta, w_g, w_mask, qkv_w, proj_w, proj_b,
                        ffn_kernel, ffn_bias, input_scale, kernel_scale, out):
    ctx = ExitStack()
    with ctx:
        def sb(name, shape, dt=F32):
            return ctx.enter_context(nc.sbuf_tensor(name, shape, dt))

        def sem(name):
            return ctx.enter_context(nc.semaphore(name))

        phi_w = sb("phi_w", [INTER, C])
        theta_w = sb("theta_w", [INTER, C])
        g_w = sb("g_w", [INTER, C])
        mask_w = sb("mask_w", [C, INTER])
        mask_wt = sb("mask_wt", [INTER, C])
        qkv_rows = sb("qkv_rows", [C, 3, C])
        proj_rows = sb("proj_rows", [C, C])
        bilinear_t = sb("bilinear_t", [C, C])
        gmask_t = sb("gmask_t", [C, C])
        qkv_t = sb("qkv_t", [C, 3, C])
        proj_t = sb("proj_t", [C, C])
        proj_bias = sb("proj_bias", [HALF, C])
        ffn_k = sb("ffn_k", [C, C])
        ffn_kc = sb("ffn_kc", [C, C])
        ffn_ks = sb("ffn_ks", [C, C])
        k_half8 = sb("k_half8", [C, C], FP8)
        k_tiny8 = sb("k_tiny8", [C, C], FP8)
        k_tinyhalf8 = sb("k_tinyhalf8", [C, C], FP8)
        k_part = sb("k_part", [C, 2, C])
        kq = sb("kq", [C, C], BF16)
        kq_twice = sb("kq_twice", [C, C], BF16)
        kq_minus = sb("kq_minus", [C, C], BF16)
        bias_raw = sb("bias_raw", [C, 1])
        bias_bf = sb("bias_bf", [C, 1], BF16)
        bias_col = sb("bias_col", [C, 1])
        scales = sb("scales", [C, 2])
        scale_inv = sb("scale_inv", [C, 2])
        scale_prod = sb("scale_prod", [C, 1])
        identity = sb("identity", [C, C])
        head_mask = sb("head_mask", [C, HEADS])
        parity_mask = sb("parity_mask", [C, 2])
        query_sel = sb("query_sel", [QW, HEADS, QW], BF16)
        wide_mask = sb("wide_mask", [QW, WINDOWS, KW], BF16)
        narrow_rows = sb("narrow_rows", [QW, KW], BF16)
        narrow_mask = sb("narrow_mask", [C, KW])
        minus_half = sb("minus_half", [HALF, 2])
        ln_eps = sb("ln_eps", [HALF, 2])

        t_all = sb("t_all", [HALF, UNITS, TOK])
        tb_all = sb("tb_all", [HALF, UNITS, TOK])
        out_all = sb("out_all", [C, UNITS, TOK])

        x_cur = sb("x_cur", [C, TOK])
        u_sb = sb("u_sb", [C, TOK])
        col_nmax = sb("col_nmax", [HALF, 1])
        col_sum = sb("col_sum", [HALF, 1])
        col_inv = sb("col_inv", [HALF, 1])
        e_sb = sb("e_sb", [HALF, HALF])
        g_sb = sb("g_sb", [HALF, TOK])
        st1 = sb("st1", [HALF, 2, 6])
        mv1 = sb("mv1", [HALF, 2, 2])
        ve1 = sb("ve1", [HALF, 2])
        rstd1 = sb("rstd1", [HALF, 2])
        z_sb = sb("z_sb", [HALF, TOK])
        zt_sb = sb("zt_sb", [C, TOK])
        q_pair = sb("q_pair", [C, WINDOWS, 2, QW])
        k_pad = sb("k_pad", [C, PADDED])
        v_pad = sb("v_pad", [C, PADDED])
        v_win = sb("v_win", [C, WINDOWS, QUAD])
        row_max = sb("row_max", [C, BANKS, KINDS, WB])
        row_sum = sb("row_sum", [C, BANKS, KINDS, WB])
        row_inv = sb("row_inv", [C, BANKS, KINDS, WB])
        narrow = sb("narrow", [C, BANKS, WB, KW])
        diff = sb("diff", [C, BANKS, KINDS, WB, KW])
        expd = sb("expd", [C, BANKS, KINDS, WB, KW])
        prob2 = sb("prob2", [C, BANKS, KINDS, WB, KW])
        prob = sb("prob", [C, BANKS, WB, KW])
        prob_t = sb("prob_t", [C, BANKS, WB, QUAD])
        att_even = sb("att_even", [C, WINDOWS, QW])
        att_t = sb("att_t", [C, WINDOWS, QW])
        t2_sb = sb("t2_sb", [HALF, TOK])
        st2 = sb("st2", [HALF, 2, 6])
        mv2 = sb("mv2", [HALF, 2, 2])
        ve2 = sb("ve2", [HALF, 2])
        rstd2 = sb("rstd2", [HALF, 2])
        z2_sb = sb("z2_sb", [HALF, TOK])
        t2b = sb("t2b", [C, TOK])
        y_sb = sb("y_sb", [C, TOK])
        y_tiny = sb("y_tiny", [C, TOK])
        y_half8 = sb("y_half8", [C, TOK], FP8)
        y_tiny8 = sb("y_tiny8", [C, TOK], FP8)
        y_tinyhalf8 = sb("y_tinyhalf8", [C, TOK], FP8)

        bank = [ctx.enter_context(nc.psum_tensor(f"bank{i}", [128, 512], F32)) for i in range(8)]
        ps_u, ps_attn, ps_zt = bank[0][:, 0:TOK], bank[0][:, 0:HALF], bank[0][:, 0:TOK]
        ps_g, ps_t = bank[1][:, 0:TOK], bank[1][:, 0:TOK]
        ps_q, ps_k = bank[2][:, 0:TOK], bank[2][:, TOK:2 * TOK]
        ps_v = bank[3][:, 0:TOK]
        ps_scores = [bank[4 + g][:, 0:WB * KW].rearrange("p (w n) -> p w n", w=WB) for g in range(BANKS)]
        ps_pv, ps_z2t, ps_t2t = bank[6][:, :], bank[6][:, 0:TOK], bank[6][:, TOK:2 * TOK]
        ps_proj, ps_ffn = bank[7][:, 0:TOK], bank[7][:, 0:TOK]

        bilinear_in, gmask_in, qkv_in, proj_in = sem("bilinear_in"), sem("gmask_in"), sem("qkv_in"), sem("proj_in")
        ffn_in = sem("ffn_in")
        pool_const = sem("pool_const")
        identity_made, masks_made, heads_made, zeros_made = (
            sem("identity_made"), sem("masks_made"), sem("heads_made"), sem("zeros_made"))
        weight_mm, weight_done = sem("weight_mm"), sem("weight_done")
        quant_step, parity_made, kernel_done = sem("quant_step"), sem("parity_made"), sem("kernel_done")
        mask_kept = sem("mask_kept")

        x_in = sem("x_in")
        u_mm, u_done = sem("u_mm"), sem("u_done")
        attn_mm, g_mm = sem("attn_mm"), sem("g_mm")
        nmax_done, e_done, inv_done, g_done = sem("nmax_done"), sem("e_done"), sem("inv_done"), sem("g_done")
        t_mm, t_kept = sem("t_mm"), sem("t_kept")
        stats1, aggr1, var1, rstd1_done = sem("stats1"), sem("aggr1"), sem("var1"), sem("rstd1_done")
        z_done, zt_mm, zt_done = sem("z_done"), sem("zt_mm"), sem("zt_done")
        qkv_mm, v_done, qk_done, vwin_done = sem("qkv_mm"), sem("v_done"), sem("qk_done"), sem("vwin_done")
        tb_done = sem("tb_done")
        scores_mm = [sem(f"scores_mm{g}") for g in range(BANKS)]
        narrow_done = [sem(f"narrow_done{g}") for g in range(BANKS)]
        max_done = [sem(f"max_done{g}") for g in range(BANKS)]
        diff_done = [sem(f"diff_done{g}") for g in range(BANKS)]
        exp_done = [sem(f"exp_done{g}") for g in range(BANKS)]
        sum_done = [sem(f"sum_done{g}") for g in range(BANKS)]
        rinv_done = [sem(f"rinv_done{g}") for g in range(BANKS)]
        scaled = [sem(f"scaled{g}") for g in range(BANKS)]
        prob_done = [sem(f"prob_done{g}") for g in range(BANKS)]
        probt_done = [sem(f"probt_done{g}") for g in range(BANKS)]
        pv_mm, even_done, att_done = sem("pv_mm"), sem("even_done"), sem("att_done")
        proj_mm, t2_done = sem("proj_mm"), sem("t2_done")
        stats2, aggr2, var2, rstd2_done = sem("stats2"), sem("aggr2"), sem("var2"), sem("rstd2_done")
        z2_done, z2t_mm, t2b_done = sem("z2_done"), sem("z2t_mm"), sem("t2b_done")
        y_done, yhalf_done, ytiny_done = sem("y_done"), sem("yhalf_done"), sem("ytiny_done")
        tiny8_done, ffn_mm, out_done, out_sent = sem("tiny8_done"), sem("ffn_mm"), sem("out_done"), sem("out_sent")

        def wait(engine, s, units):
            if not (isinstance(units, int) and units <= 0):
                engine.wait_ge(s, units)

        def part(engine):
            engine.wait_ge(zeros_made, 1)

        def pipeline(engine, step):
            for k in range(3):
                step(k, True, k >= 1, k >= 2)
            with engine.Fori(3, UNITS) as k:
                step(k, True, True, True)
            step(UNITS, False, True, True)
            step(UNITS + 1, False, False, True)

        block = ctx.enter_context(nc.Block())

        @block.sync
        def _(sp):
            sp.dma_start(x_cur[:, :], x[0]).then_inc(x_in, 16)
            sp.dma_start(g_w[:, :], w_g).then_inc(gmask_in, 16)
            sp.dma_start(mask_w[:, :], w_mask).then_inc(gmask_in, 16)
            sp.dma_start(qkv_rows[:, :, :], qkv_w.rearrange("(t o) c -> o t c", t=3)).then_inc(qkv_in, 16)

            def load(u):
                sp.wait_ge(t_mm, u)
                sp.dma_start(x_cur[:, :], x[u]).then_inc(x_in, 16)

            def store(u):
                sp.wait_ge(out_done, u + 1)
                sp.dma_start(out[u], out_all[:, u, :]).then_inc(out_sent, 16)

            load(1)
            load(2)
            with sp.Fori(3, UNITS) as u:
                load(u)
                store(u - 3)
            for u in range(UNITS - 3, UNITS):
                store(u)
            sp.wait_ge(out_sent, 16 * UNITS)

        @block.tensor
        def _(pe):
            mm = nc.tensor.matmul

            pe.wait_ge(bilinear_in, 32)
            mm(bank[0][:, 0:C], theta_w[:, :], phi_w[:, :], start=True, stop=True).then_inc(weight_mm, 1)
            pe.wait_ge(identity_made, 1)
            pe.wait_ge(gmask_in, 32)
            nc.tensor.transpose(bank[1][0:INTER, 0:C], mask_w[:, :], identity[:, :]).then_inc(weight_mm, 1)
            pe.wait_ge(qkv_in, 16)
            for i in range(3):
                nc.tensor.transpose(bank[3][:, i * C:(i + 1) * C], qkv_rows[:, i, :], identity[:, :]).then_inc(weight_mm, 1)
            pe.wait_ge(proj_in, 32)
            nc.tensor.transpose(bank[3][:, 3 * C:4 * C], proj_rows[:, :], identity[:, :]).then_inc(weight_mm, 1)
            pe.wait_ge(weight_done, 2)
            mm(bank[2][:, 0:C], g_w[:, :], mask_wt[:, :], start=True, stop=True).then_inc(weight_mm, 1)
            pe.wait_ge(weight_done, 5)
            pe.wait_ge(masks_made, 1)
            pe.wait_ge(zeros_made, 1)
            mm(bank[6][:, 0:KW], query_sel[:, :, :].rearrange("p h q -> p (h q)"), narrow_rows[:, :],
               start=True, stop=True).then_inc(weight_mm, 1)

            def halves(s):
                return slice(s * HALF, (s + 1) * HALF)

            def apply_bilinear(u):
                pe.wait_ge(x_in, 16 * (u + 1))
                mm(ps_u, bilinear_t[:, :], x_cur[:, :], start=True, stop=True).then_inc(u_mm, 1)

            def attention_and_g(u):
                wait(pe, u_done, u + 1)
                for s in range(2):
                    last = mm(ps_attn, x_cur[:, halves(s)], u_sb[:, halves(s)], start=(s == 0), stop=(s == 1))
                last.then_inc(attn_mm, 1)
                for s in range(2):
                    last = mm(ps_g[:, halves(s)], x_cur[:, halves(s)], gmask_t[:, :], start=True, stop=True)
                last.then_inc(g_mm, 1)

            def mix_tokens(u):
                wait(pe, e_done, u + 1)
                wait(pe, g_done, u + 1)
                for s in range(2):
                    mm(ps_t[:, halves(s)], x_cur[:, halves(s)], identity[:, :], start=(s == 0), stop=False,
                       is_transpose=True)
                mm(ps_t, e_sb[:, :], g_sb[:, :], start=False, stop=True).then_inc(t_mm, 1)

            def turn_z(u):
                wait(pe, z_done, u + 1)
                for s in range(2):
                    last = nc.tensor.transpose(ps_zt[:, halves(s)], z_sb[:, halves(s)], identity[:, :])
                last.then_inc(zt_mm, 1)

            def project_qkv(u):
                wait(pe, zt_done, u + 1)
                wait(pe, qk_done, u)
                for i, o in ((1, ps_k), (2, ps_v), (0, ps_q)):
                    last = mm(o, qkv_t[:, i, :], zt_sb[:, :], start=True, stop=True)
                last.then_inc(qkv_mm, 1)

            def scores(u, g):
                if g == 0:
                    wait(pe, qk_done, u + 1)
                wait(pe, diff_done[g], u)
                mm(bank[4 + g][:, 0:WB * KW], query_sel[:, :, :].rearrange("p h q -> p (h q)"),
                   wide_mask[:, g * WB:(g + 1) * WB, :].rearrange("p w n -> p (w n)"), start=True, stop=False)
                for w in range(WB):
                    at = (g * WB + w) * QW
                    for i in range(PAIRS):
                        q = slice(QUAD * i, QUAD * (i + 1))
                        last = mm(ps_scores[g][q, w, :],
                                  q_pair[q, g * WB + w, :, :].rearrange("p e q -> p (e q)"),
                                  k_pad[q, at:at + KW], start=False, stop=(w == WB - 1))
                last.then_inc(scores_mm[g], 1)

            def weigh_values(u):
                for g in range(BANKS):
                    part(pe)
                    if g == 0:
                        wait(pe, vwin_done, u + 1)
                    wait(pe, probt_done[g], u + 1)
                    for w in range(WB):
                        at = (g * WB + w) * QUAD
                        for i in range(PAIRS):
                            q = slice(QUAD * i, QUAD * (i + 1))
                            last = mm(ps_pv[q, at:at + QUAD], v_win[q, g * WB + w, :], prob_t[q, g, w, :],
                                      start=True, stop=True)
                last.then_inc(pv_mm, 1)

            def project(u):
                wait(pe, att_done, u + 1)
                a = att_t[:, :, :].rearrange("p w q -> p (w q)")
                for s in range(2):
                    last = mm(ps_proj[:, halves(s)], a[:, halves(s)], proj_t[:, :], start=True, stop=True)
                last.then_inc(proj_mm, 1)

            def turn_back(u):
                wait(pe, z2_done, u + 1)
                for s in range(2):
                    nc.tensor.transpose(ps_z2t[:, halves(s)], z2_sb[:, halves(s)], identity[:, :])
                for s in range(2):
                    last = nc.tensor.transpose(ps_t2t[:, halves(s)], t2_sb[:, halves(s)], identity[:, :])
                last.then_inc(z2t_mm, 1)

            def feed_forward(u):
                part(pe)
                if isinstance(u, int) and u == 0:
                    pe.wait_ge(kernel_done, 3)
                wait(pe, yhalf_done, u + 1)
                wait(pe, tiny8_done, u + 1)
                mm(ps_ffn, kq_twice[:, :], y_half8[:, :], start=True, stop=False)
                mm(ps_ffn, kq[:, :], y_tiny8[:, :], start=False, stop=False)
                mm(ps_ffn, kq_minus[:, :], y_tinyhalf8[:, :], start=False, stop=True).then_inc(ffn_mm, 1)

            def step(k, a, b, c):
                if a:
                    apply_bilinear(k)
                if b:
                    scores(k - 1, 0)
                if a:
                    attention_and_g(k)
                if b:
                    scores(k - 1, 1)
                if c:
                    weigh_values(k - 2)
                if a:
                    mix_tokens(k)
                if c:
                    project(k - 2)
                if a:
                    turn_z(k)
                if c:
                    turn_back(k - 2)
                if a:
                    project_qkv(k)
                if c:
                    feed_forward(k - 2)

            pipeline(pe, step)

        @block.scalar
        def _(act):
            act.dma_start(theta_w[:, :], w_theta).then_inc(bilinear_in, 16)
            act.dma_start(phi_w[:, :], w_phi).then_inc(bilinear_in, 16)
            act.dma_start(proj_rows[:, :], proj_w).then_inc(proj_in, 16)
            act.dma_start(proj_bias[:, :], proj_b.unsqueeze(0).to_broadcast([HALF, C])).then_inc(proj_in, 16)
            act.dma_start(ffn_k[:, :], ffn_kernel).then_inc(ffn_in, 16)
            act.dma_start(bias_raw[:, :], ffn_bias.unsqueeze(1)).then_inc(ffn_in, 16)
            act.dma_start(scales[:, 0:1], input_scale.unsqueeze(0).to_broadcast([C, 1])).then_inc(ffn_in, 16)
            act.dma_start(scales[:, 1:2], kernel_scale.unsqueeze(0).to_broadcast([C, 1])).then_inc(ffn_in, 16)
            nc.scalar.preload_act_table(ACT.Exp)

            act.wait_ge(weight_mm, 1)
            nc.scalar.copy(bilinear_t[:, :], bank[0][:, 0:C]).then_inc(weight_done, 1)
            act.wait_ge(weight_mm, 2)
            nc.scalar.copy(mask_wt[:, :], bank[1][0:INTER, 0:C]).then_inc(weight_done, 1)
            act.wait_ge(weight_mm, 6)
            nc.scalar.copy(qkv_t[:, :, :].rearrange("p t c -> p (t c)"), bank[3][:, 0:3 * C]).then_inc(weight_done, 1)
            nc.scalar.copy(proj_t[:, :], bank[3][:, 3 * C:4 * C]).then_inc(weight_done, 1)
            act.wait_ge(weight_mm, 7)
            nc.scalar.copy(gmask_t[:, :], bank[2][:, 0:C]).then_inc(weight_done, 1)
            act.wait_ge(parity_made, 1)
            act.wait_ge(zeros_made, 1)

            def copy_u(u):
                wait(act, u_mm, u + 1)
                wait(act, attn_mm, u)
                nc.scalar.copy(u_sb[:, :], ps_u).then_inc(u_done, 1)

            def column_exp(u):
                wait(act, nmax_done, u + 1)
                wait(act, t_mm, u)
                nc.scalar.activation(e_sb[:, :], ps_attn, ACT.Exp, bias=col_nmax[:, 0:1], scale=1.0,
                                     accum_out=col_sum[:, 0:1]).then_inc(e_done, 1)

            def scale_g(u):
                wait(act, g_mm, u + 1)
                wait(act, inv_done, u + 1)
                nc.scalar.activation(g_sb[:, :], ps_g, ACT.Copy, scale=col_inv[:, 0:1]).then_inc(g_done, 1)

            def keep_t(u):
                wait(act, t_mm, u + 1)
                nc.scalar.copy(t_all[:, u, :], ps_t).then_inc(t_kept, 1)

            def copy_zt(u):
                wait(act, zt_mm, u + 1)
                nc.scalar.copy(zt_sb[:, :], ps_zt).then_inc(zt_done, 1)

            def copy_qkv(u):
                wait(act, qkv_mm, u + 1)
                wait(act, vwin_done, u)
                nc.scalar.mul(v_pad[:, PAD:PAD + TOK], ps_v, 1.0 / KINDS).then_inc(v_done, 1)
                wait(act, scores_mm[1], u)
                nc.scalar.copy(k_pad[:, PAD:PAD + TOK], ps_k)
                for e in range(2):
                    last = nc.scalar.activation(q_pair[:, :, e, :], ps_q.rearrange("p (w q) -> p w q", q=QW),
                                                ACT.Copy, scale=parity_mask[:, e:e + 1])
                last.then_inc(qk_done, 1)

            def band_exp(u, g):
                wait(act, diff_done[g], u + 1)
                wait(act, scaled[g], u)
                wait(act, sum_done[g], u)
                nc.scalar.activation(expd[:, g].rearrange("p k w n -> p (k w n)"),
                                     diff[:, g].rearrange("p k w n -> p (k w n)"),
                                     ACT.Exp, scale=SCALE).then_inc(exp_done[g], 1)

            def pick_even(u):
                wait(act, pv_mm, u + 1)
                wait(act, att_done, u)
                nc.scalar.activation(att_even[:, :, :],
                                     ps_pv.rearrange("p (w e q) -> p w e q", e=2, q=QW)[:, :, 0, :],
                                     ACT.Copy, scale=parity_mask[:, 0:1]).then_inc(even_done, 1)

            def add_bias(u):
                if isinstance(u, int) and u == 0:
                    act.wait_ge(quant_step, 2)
                wait(act, z2t_mm, u + 1)
                wait(act, y_done, u + 1)
                wait(act, out_done, u)
                nc.scalar.activation(t2b[:, :], ps_t2t, ACT.Identity, bias=bias_col[:, 0:1],
                                     scale=1.0).then_inc(t2b_done, 1)

            def tiny_to_fp8(u):
                part(act)
                wait(act, ytiny_done, u + 1)
                wait(act, ffn_mm, u)
                nc.scalar.activation(y_tiny8[:, :], y_tiny[:, :], ACT.Copy, saturate=False)
                nc.scalar.activation(y_tinyhalf8[:, :], y_tiny[:, :], ACT.Copy, scale=0.5,
                                     saturate=False).then_inc(tiny8_done, 1)

            def step(k, a, b, c):
                if a:
                    copy_u(k)
                if b:
                    band_exp(k - 1, 0)
                if a:
                    column_exp(k)
                    scale_g(k)
                if b:
                    band_exp(k - 1, 1)
                if c:
                    pick_even(k - 2)
                if a:
                    keep_t(k)
                    copy_zt(k)
                if c:
                    add_bias(k - 2)
                    tiny_to_fp8(k - 2)
                if a:
                    copy_qkv(k)

            pipeline(act, step)

        @block.vector
        def _(dve):
            v = nc.vector
            dve.wait_ge(weight_mm, 8)
            v.tensor_copy(narrow_mask[:, :], bank[6][:, 0:KW]).then_inc(mask_kept, 1)

            dve.wait_ge(heads_made, 1)
            v.tensor_reduce(parity_mask[:, :], head_mask[:, :].rearrange("p (i e) -> p e i", e=2),
                            AX.X, ALU.add).then_inc(parity_made, 1)

            def quantise_kernel():
                dve.wait_ge(ffn_in, 64)
                v.tensor_copy(bias_bf[:, :], bias_raw[:, :]).then_inc(quant_step, 1)
                dve.wait_ge(quant_step, 1)
                v.tensor_copy(bias_col[:, :], bias_bf[:, :]).then_inc(quant_step, 1)
                v.reciprocal(scale_inv[:, :], scales[:, :]).then_inc(quant_step, 1)
                v.tensor_tensor(scale_prod[:, :], scales[:, 0:1], scales[:, 1:2], ALU.mult).then_inc(quant_step, 1)
                dve.wait_ge(quant_step, 4)
                v.tensor_scalar(ffn_ks[:, :], ffn_k[:, :], scale_inv[:, 1:2], E4M3_MAX, ALU.mult, ALU.min).then_inc(quant_step, 1)
                dve.wait_ge(quant_step, 5)
                v.tensor_scalar(k_half8[:, :], ffn_ks[:, :], -E4M3_MAX, 0.5, ALU.max, ALU.mult, saturate=False).then_inc(quant_step, 1)
                v.tensor_scalar(ffn_kc[:, :], ffn_ks[:, :], TINY, -TINY, ALU.min, ALU.max).then_inc(quant_step, 1)
                dve.wait_ge(quant_step, 7)
                v.tensor_scalar(k_tiny8[:, :], ffn_kc[:, :], 1.0, None, ALU.mult, saturate=False).then_inc(quant_step, 1)
                v.tensor_scalar(k_tinyhalf8[:, :], ffn_kc[:, :], 0.5, None, ALU.mult, saturate=False).then_inc(quant_step, 1)
                dve.wait_ge(quant_step, 9)
                v.scalar_tensor_tensor(k_part[:, 0, :], k_tinyhalf8[:, :], -2.0, k_tiny8[:, :],
                                       ALU.mult, ALU.add).then_inc(quant_step, 1)
                dve.wait_ge(quant_step, 10)
                v.scalar_tensor_tensor(k_part[:, 1, :], k_half8[:, :], 2.0, k_part[:, 0, :],
                                       ALU.mult, ALU.add).then_inc(quant_step, 1)
                dve.wait_ge(quant_step, 11)
                v.tensor_copy(kq[:, :], k_part[:, 1, :]).then_inc(kernel_done, 1)
                v.tensor_scalar(kq_twice[:, :], k_part[:, 1, :], 2.0, None, ALU.mult).then_inc(kernel_done, 1)
                v.tensor_scalar(kq_minus[:, :], k_part[:, 1, :], -2.0, None, ALU.mult).then_inc(kernel_done, 1)

            def halves(s):
                return slice(s * HALF, (s + 1) * HALF)

            def column_max(u):
                wait(dve, attn_mm, u + 1)
                v.tensor_reduce(col_nmax[:, :], ps_attn, AX.X, ALU.max, negate=True).then_inc(nmax_done, 1)

            def column_inverse(u):
                wait(dve, e_done, u + 1)
                wait(dve, g_done, u)
                v.reciprocal(col_inv[:, :], col_sum[:, :]).then_inc(inv_done, 1)

            def stats_first(u):
                wait(dve, t_kept, u + 1)
                v.bn_stats(st1[:, 0, :], t_all[:, u, halves(0)])
                v.bn_stats(st1[:, 1, :], t_all[:, u, halves(1)]).then_inc(stats1, 1)
                part(dve)
                wait(dve, stats1, u + 1)
                v.bn_aggr(mv1[:, 0, :], st1[:, 0, :])
                v.bn_aggr(mv1[:, 1, :], st1[:, 1, :]).then_inc(aggr1, 1)

            def norm_first(u):
                wait(dve, rstd1_done, u + 1)
                wait(dve, zt_mm, u)
                for s in range(2):
                    last = v.tensor_scalar(z_sb[:, halves(s)], t_all[:, u, halves(s)], mv1[:, s, 0:1],
                                           rstd1[:, s:s + 1], ALU.subtract, ALU.mult)
                last.then_inc(z_done, 1)

            def window_values(u):
                wait(dve, v_done, u + 1)
                wait(dve, pv_mm, u)
                windows = bass.AP(v_pad, 0, [[PADDED, C], [QW, WINDOWS], [1, KW]])
                v.transpose(v_win[:, :, :], windows).then_inc(vwin_done, 1)

            def subtract_max(u, g):
                wait(dve, scores_mm[g], u + 1)
                v.tensor_reduce(row_max[:, g, 1, :], ps_scores[g], AX.X, ALU.max)
                v.tensor_tensor(narrow[:, g], ps_scores[g], narrow_mask[:, :].unsqueeze(1).to_broadcast([C, WB, KW]),
                                ALU.add).then_inc(narrow_done[g], 1)
                wait(dve, narrow_done[g], u + 1)
                v.tensor_reduce(row_max[:, g, 0, :], narrow[:, g], AX.X, ALU.max).then_inc(max_done[g], 1)
                wait(dve, exp_done[g], u)
                v.tensor_tensor(diff[:, g, 1], ps_scores[g],
                                row_max[:, g, 1].unsqueeze(2).to_broadcast([C, WB, KW]), ALU.subtract)
                wait(dve, max_done[g], u + 1)
                v.tensor_tensor(diff[:, g, 0], narrow[:, g],
                                row_max[:, g, 0].unsqueeze(2).to_broadcast([C, WB, KW]),
                                ALU.subtract).then_inc(diff_done[g], 1)

            def row_sums(u, g):
                wait(dve, exp_done[g], u + 1)
                v.tensor_reduce(row_sum[:, g], expd[:, g], AX.X, ALU.add).then_inc(sum_done[g], 1)
                wait(dve, sum_done[g], u + 1)
                wait(dve, scaled[g], u)
                v.reciprocal(row_inv[:, g], row_sum[:, g]).then_inc(rinv_done[g], 1)

            def turn_probs(u, g):
                wait(dve, prob_done[g], u + 1)
                wait(dve, pv_mm, u)
                v.transpose(prob_t[:, g].rearrange("p w n -> p (w n)"),
                            prob[:, g].rearrange("p w n -> p (w n)")).then_inc(probt_done[g], 1)

            def pick_odd(u):
                wait(dve, even_done, u + 1)
                wait(dve, proj_mm, u)
                v.scalar_tensor_tensor(att_t[:, :, :], ps_pv.rearrange("p (w e q) -> p w e q", e=2, q=QW)[:, :, 1, :],
                                       parity_mask[:, 1:2], att_even[:, :, :], ALU.mult, ALU.add).then_inc(att_done, 1)

            def residual(u):
                wait(dve, proj_mm, u + 1)
                wait(dve, tb_done, u + 1)
                wait(dve, z2t_mm, u)
                v.tensor_tensor(t2_sb[:, :], ps_proj, tb_all[:, u, :], ALU.add).then_inc(t2_done, 1)

            def stats_second(u):
                wait(dve, t2_done, u + 1)
                v.bn_stats(st2[:, 0, :], t2_sb[:, halves(0)])
                v.bn_stats(st2[:, 1, :], t2_sb[:, halves(1)]).then_inc(stats2, 1)
                part(dve)
                wait(dve, stats2, u + 1)
                v.bn_aggr(mv2[:, 0, :], st2[:, 0, :])
                v.bn_aggr(mv2[:, 1, :], st2[:, 1, :]).then_inc(aggr2, 1)

            def norm_second(u):
                wait(dve, rstd2_done, u + 1)
                for s in range(2):
                    last = v.tensor_scalar(z2_sb[:, halves(s)], t2_sb[:, halves(s)], mv2[:, s, 0:1],
                                           rstd2[:, s:s + 1], ALU.subtract, ALU.mult)
                last.then_inc(z2_done, 1)

            def quantise(u):
                wait(dve, z2t_mm, u + 1)
                wait(dve, tiny8_done, u)
                wait(dve, ffn_mm, u)
                v.tensor_scalar(y_sb[:, :], ps_z2t, scale_inv[:, 0:1], E4M3_MAX, ALU.mult, ALU.min).then_inc(y_done, 1)
                wait(dve, y_done, u + 1)
                v.tensor_scalar(y_tiny[:, :], y_sb[:, :], TINY, -TINY, ALU.min, ALU.max).then_inc(ytiny_done, 1)
                v.tensor_scalar(y_half8[:, :], y_sb[:, :], -E4M3_MAX, 0.5, ALU.max, ALU.mult,
                                saturate=False).then_inc(yhalf_done, 1)

            def result(u):
                wait(dve, ffn_mm, u + 1)
                wait(dve, t2b_done, u + 1)
                v.scalar_tensor_tensor(out_all[:, u, :], ps_ffn, scale_prod[:, 0:1], t2b[:, :],
                                       ALU.mult, ALU.add).then_inc(out_done, 1)

            def step(k, a, b, c):
                if b:
                    subtract_max(k - 1, 0)
                if a:
                    column_max(k)
                    column_inverse(k)
                if b:
                    subtract_max(k - 1, 1)
                    row_sums(k - 1, 0)
                if c:
                    pick_odd(k - 2)
                if b:
                    window_values(k - 1)
                if a:
                    stats_first(k)
                if b:
                    row_sums(k - 1, 1)
                if c:
                    residual(k - 2)
                    stats_second(k - 2)
                if a:
                    norm_first(k)
                if b:
                    turn_probs(k - 1, 0)
                if c:
                    norm_second(k - 2)
                    quantise(k - 2)
                if b:
                    turn_probs(k - 1, 1)
                if c:
                    result(k - 2)
                if isinstance(k, int) and k == 0:
                    quantise_kernel()

            pipeline(dve, step)

        @block.gpsimd
        def _(pool):
            p = nc.gpsimd

            p.memset(identity[:, :], 0.0).then_inc(pool_const, 1)
            pool.wait_ge(pool_const, 1)
            p.affine_select(out=identity[:, :], in_=identity[:, :], compare_op=ALU.not_equal, fill=1.0, base=0,
                            pattern=[[-1, C]], channel_multiplier=1).then_inc(identity_made, 1)
            p.memset(head_mask[:, :], 1.0).then_inc(pool_const, 1)
            steps = 2
            for sign in (1, -1):
                pool.wait_ge(pool_const, steps)
                p.affine_select(out=head_mask[:, :], in_=head_mask[:, :], compare_op=ALU.is_ge, fill=0.0,
                                base=0 if sign == 1 else D - 1, pattern=[[-sign * D, HEADS]],
                                channel_multiplier=sign).then_inc(pool_const, 1)
                steps += 1
            pool.wait_ge(pool_const, steps)
            p.memset(query_sel[:, :, :], 0.0).then_inc(heads_made, 1)
            pool.wait_ge(heads_made, 1)
            p.affine_select(out=query_sel[:, :, :], in_=query_sel[:, :, :], compare_op=ALU.not_equal, fill=1.0, base=0,
                            pattern=[[0, HEADS], [-1, QW]], channel_multiplier=1).then_inc(pool_const, 1)
            p.memset(wide_mask[:, :, :], 0.0).then_inc(pool_const, 1)
            p.memset(narrow_rows[:, :], 0.0).then_inc(pool_const, 1)
            steps += 3
            pool.wait_ge(pool_const, steps)
            for sign in (1, -1):
                for m, r, pattern in ((narrow_rows[:, :], RADIUS[0], [[sign, KW]]),
                                      (wide_mask[:, :, :], RADIUS[1], [[0, WINDOWS], [sign, KW]])):
                    p.affine_select(out=m, in_=m, compare_op=ALU.is_ge, fill=NEG, base=r - sign * PAD,
                                    pattern=pattern, channel_multiplier=-sign).then_inc(pool_const, 1)
                    steps += 1
                    pool.wait_ge(pool_const, steps)
            m = wide_mask[:, 0, 0:PAD]
            p.memset(m, NEG)
            m = wide_mask[:, WINDOWS - 1, KW - PAD:KW]
            p.memset(m, NEG).then_inc(masks_made, 1)
            p.memset(k_pad[:, 0:PAD], 0.0)
            p.memset(k_pad[:, PAD + TOK:PADDED], 0.0)
            p.memset(v_pad[:, 0:PAD], 0.0)
            p.memset(v_pad[:, PAD + TOK:PADDED], 0.0).then_inc(zeros_made, 1)
            p.memset(minus_half[:, :], -0.5)
            p.memset(ln_eps[:, :], LN_EPS).then_inc(pool_const, 1)
            pool.wait_ge(pool_const, steps + 1)

            def rstd_first(u):
                wait(pool, aggr1, u + 1)
                p.tensor_tensor(ve1[:, :], mv1[:, :, 1], ln_eps[:, :], ALU.add).then_inc(var1, 1)
                wait(pool, var1, u + 1)
                p.tensor_tensor(rstd1[:, :], ve1[:, :], minus_half[:, :], ALU.pow).then_inc(rstd1_done, 1)

            def rstd_second(u):
                wait(pool, aggr2, u + 1)
                p.tensor_tensor(ve2[:, :], mv2[:, :, 1], ln_eps[:, :], ALU.add).then_inc(var2, 1)
                wait(pool, var2, u + 1)
                p.tensor_tensor(rstd2[:, :], ve2[:, :], minus_half[:, :], ALU.pow).then_inc(rstd2_done, 1)

            def add_proj_bias(u):
                wait(pool, t_kept, u + 1)
                b = proj_bias[:, :].unsqueeze(1).to_broadcast([HALF, 2, C])
                p.tensor_tensor(tb_all[:, u, :].rearrange("p (s c) -> p s c", s=2),
                                t_all[:, u, :].rearrange("p (s c) -> p s c", s=2), b, ALU.add).then_inc(tb_done, 1)

            def scale_probs(u, g):
                wait(pool, rinv_done[g], u + 1)
                p.tensor_tensor(prob2[:, g], expd[:, g],
                                row_inv[:, g].unsqueeze(3).to_broadcast([C, KINDS, WB, KW]), ALU.mult).then_inc(scaled[g], 1)
                wait(pool, scaled[g], u + 1)
                wait(pool, probt_done[g], u)
                p.tensor_tensor(prob[:, g], prob2[:, g, 0], prob2[:, g, 1], ALU.add).then_inc(prob_done[g], 1)

            def step(k, a, b, c):
                if b:
                    add_proj_bias(k - 1)
                    scale_probs(k - 1, 0)
                if a:
                    rstd_first(k)
                if b:
                    scale_probs(k - 1, 1)
                if c:
                    rstd_second(k - 2)

            pool.wait_ge(proj_in, 32)
            pipeline(pool, step)


_INS = ['x', 'L0_conv_w_phi', 'L0_conv_w_theta', 'L0_conv_w_g', 'L0_conv_w_mask', 'L1_attn_qkv_w',
        'L1_attn_proj_w', 'L1_attn_proj_b', 'L1_ffn_kernel', 'L1_ffn_bias', 'L1_ffn_input_scale',
        'L1_ffn_kernel_scale']


def kernel(**inputs):
    import numpy as _np
    import concourse.bacc as _bacc
    from concourse import mybir as _mybir
    from concourse.bass_utils import run_bass_kernel_spmd as _run

    nc = _bacc.Bacc("TRN2", target_bir_lowering=False, num_devices=1)
    arrays, args = {}, []
    for name in _INS:
        a = _np.ascontiguousarray(inputs[name])
        shape = a.shape
        if name == 'x':
            a = a.reshape(UNITS, C, TOK)
        arrays[f"in_{name}_dram"] = a
        args.append(nc.dram_tensor(f"in_{name}_dram", a.shape, _mybir.dt.from_np(a.dtype), kind="ExternalInput").ap())
    args.append(nc.dram_tensor("out_0_dram", (UNITS, C, TOK), _mybir.dt.float32, kind="ExternalOutput").ap())
    hybrid_block_kernel(nc, *args)
    r = _run(nc, [arrays], core_ids=[0])
    return _np.asarray(r.results[0]["out_0_dram"]).reshape(UNITS, C, 16, 16)
```

```python
from contextlib import ExitStack

import concourse.bass as bass
from concourse import mybir


F32 = mybir.dt.float32
BF16 = mybir.dt.bfloat16
FP8 = mybir.dt.float8e4
ALU = mybir.AluOpType
ACT = mybir.ActivationFunctionType
AX = mybir.AxisListType

UNITS = 8
C = 128
HALF = 128
TOK = 2 * HALF
INTER = 64
HEADS = 8
PAIRS = HEADS // 2
D = C // HEADS
RADIUS = (4, 8)
KINDS = len(RADIUS)
QW = C // HEADS
KW = QW + 2 * RADIUS[1]
NW = QW + 2 * RADIUS[0]
NARROW = RADIUS[1] - RADIUS[0]
WINDOWS = TOK // QW
BANKS = 2
WB = WINDOWS // BANKS
PAD = RADIUS[1]
PADDED = PAD + TOK + PAD
SCALE = float(D) ** -0.5
NEG = -1.0e37
LN_EPS = 1e-5
E4M3_MAX = 448.0
LAST = 3
TINY = 2.0 ** -5
QUAD = 2 * D


def hybrid_block_kernel(nc, x, w_phi, w_theta, w_g, w_mask, qkv_w, proj_w, proj_b,
                        ffn_kernel, ffn_bias, input_scale, kernel_scale, out):
    ctx = ExitStack()
    with ctx:
        def sb(name, shape, dt=F32):
            return ctx.enter_context(nc.sbuf_tensor(name, shape, dt))

        def sem(name):
            return ctx.enter_context(nc.semaphore(name))

        phi_w = sb("phi_w", [INTER, C])
        theta_w = sb("theta_w", [INTER, C])
        g_w = sb("g_w", [INTER, C])
        mask_w = sb("mask_w", [C, INTER])
        mask_wt = sb("mask_wt", [INTER, C])
        qkv_rows = sb("qkv_rows", [C, 3, C])
        proj_rows = sb("proj_rows", [C, C])
        bilinear_t = sb("bilinear_t", [C, C])
        gmask_t = sb("gmask_t", [C, C])
        qkv_t = sb("qkv_t", [C, 3, C])
        proj_t = sb("proj_t", [C, C])
        proj_bias = sb("proj_bias", [HALF, C])
        ffn_k = sb("ffn_k", [C, C])
        ffn_kc = sb("ffn_kc", [C, C])
        ffn_ks = sb("ffn_ks", [C, C])
        k_half8 = sb("k_half8", [C, C], FP8)
        k_tiny8 = sb("k_tiny8", [C, C], FP8)
        k_tinyhalf8 = sb("k_tinyhalf8", [C, C], FP8)
        k_part = sb("k_part", [C, 2, C])
        kq = sb("kq", [C, C], BF16)
        kq_twice = sb("kq_twice", [C, C], BF16)
        kq_minus = sb("kq_minus", [C, C], BF16)
        bias_raw = sb("bias_raw", [C, 1])
        bias_bf = sb("bias_bf", [C, 1], BF16)
        bias_col = sb("bias_col", [C, 1])
        scales = sb("scales", [C, 2])
        scale_inv = sb("scale_inv", [C, 2])
        scale_prod = sb("scale_prod", [C, 1])
        identity = sb("identity", [C, C])
        head_mask = sb("head_mask", [C, HEADS])
        parity_mask = sb("parity_mask", [C, 2])
        query_sel = sb("query_sel", [QW, HEADS, QW], BF16)
        wide_mask = sb("wide_mask", [QW, WINDOWS, KW], BF16)
        narrow_rows = sb("narrow_rows", [QW, KW], BF16)
        narrow_mask = sb("narrow_mask", [C, KW])
        minus_half = sb("minus_half", [HALF, 2])
        ln_eps = sb("ln_eps", [HALF, 2])

        t_all = sb("t_all", [HALF, UNITS, TOK])
        tb_all = sb("tb_all", [HALF, UNITS, TOK])
        out_all = sb("out_all", [C, UNITS, TOK])

        x_cur = sb("x_cur", [C, TOK])
        u_sb = sb("u_sb", [C, TOK])
        col_nmax = sb("col_nmax", [HALF, 1])
        col_sum = sb("col_sum", [HALF, 1])
        col_inv = sb("col_inv", [HALF, 1])
        e_sb = sb("e_sb", [HALF, HALF])
        g_sb = sb("g_sb", [HALF, TOK])
        st1 = sb("st1", [HALF, 2, 6])
        mv1 = sb("mv1", [HALF, 2, 2])
        ve1 = sb("ve1", [HALF, 2])
        rstd1 = sb("rstd1", [HALF, 2])
        z_sb = sb("z_sb", [HALF, TOK])
        zt_sb = sb("zt_sb", [C, TOK])
        q_pair = sb("q_pair", [C, WINDOWS, 2, QW])
        k_pad = sb("k_pad", [C, PADDED])
        v_pad = sb("v_pad", [C, PADDED])
        v_win = sb("v_win", [C, WINDOWS, QUAD])
        row_max = sb("row_max", [C, BANKS, KINDS, WB])
        row_sum = sb("row_sum", [C, BANKS, KINDS, WB])
        row_inv = sb("row_inv", [C, BANKS, KINDS, WB])
        wide = sb("wide", [C, BANKS, WB, KW])
        narrow = sb("narrow", [C, BANKS, WB, NW])
        diff = sb("diff", [C, BANKS, WB * (KW + NW)])
        expd = sb("expd", [C, BANKS, WB * (KW + NW)])
        narrow_prob = sb("narrow_prob", [C, BANKS, WB, NW])
        prob = sb("prob", [C, BANKS, WB, KW])
        prob_t = sb("prob_t", [C, BANKS, WB, QUAD])
        att_even = sb("att_even", [C, WINDOWS, QW])
        att_t = sb("att_t", [C, WINDOWS, QW])
        t2_sb = sb("t2_sb", [HALF, TOK])
        st2 = sb("st2", [HALF, 2, 6])
        mv2 = sb("mv2", [HALF, 2, 2])
        ve2 = sb("ve2", [HALF, 2])
        rstd2 = sb("rstd2", [HALF, 2])
        z2_sb = sb("z2_sb", [HALF, TOK])
        t2b = sb("t2b", [C, TOK])
        y_sb = sb("y_sb", [C, TOK])
        y_tiny = sb("y_tiny", [C, TOK])
        y_half8 = sb("y_half8", [C, TOK], FP8)
        y_tiny8 = sb("y_tiny8", [C, TOK], FP8)
        y_tinyhalf8 = sb("y_tinyhalf8", [C, TOK], FP8)

        def wide_part(t, g):
            return t[:, g, 0:WB * KW].rearrange("p (w n) -> p w n", w=WB)

        def narrow_part(t, g):
            return t[:, g, WB * KW:WB * (KW + NW)].rearrange("p (w n) -> p w n", w=WB)

        bank = [ctx.enter_context(nc.psum_tensor(f"bank{i}", [128, 512], F32)) for i in range(8)]
        ps_u, ps_attn, ps_zt = bank[0][:, 0:TOK], bank[0][:, 0:HALF], bank[0][:, 0:TOK]
        ps_g, ps_t = bank[1][:, 0:TOK], bank[1][:, 0:TOK]
        ps_q, ps_k = bank[2][:, 0:TOK], bank[2][:, TOK:2 * TOK]
        ps_v = bank[3][:, 0:TOK]
        ps_scores = [bank[4 + g][:, 0:WB * KW].rearrange("p (w n) -> p w n", w=WB) for g in range(BANKS)]
        ps_pv, ps_z2t, ps_t2t = bank[6][:, :], bank[6][:, 0:TOK], bank[6][:, TOK:2 * TOK]
        ps_proj, ps_ffn = bank[7][:, 0:TOK], bank[7][:, 0:TOK]

        bilinear_in, gmask_in, qkv_in, bias_in = sem("bilinear_in"), sem("gmask_in"), sem("qkv_in"), sem("bias_in")
        ffn_in = sem("ffn_in")
        pool_const = sem("pool_const")
        identity_made, masks_made, heads_made, zeros_made = (
            sem("identity_made"), sem("masks_made"), sem("heads_made"), sem("zeros_made"))
        weight_mm, weight_done = sem("weight_mm"), sem("weight_done")
        quant_step, parity_made, kernel_done = sem("quant_step"), sem("parity_made"), sem("kernel_done")
        mask_kept = sem("mask_kept")

        x_in = sem("x_in")
        u_mm, u_done = sem("u_mm"), sem("u_done")
        attn_mm, g_mm = sem("attn_mm"), sem("g_mm")
        nmax_done, e_done, inv_done, g_done = sem("nmax_done"), sem("e_done"), sem("inv_done"), sem("g_done")
        t_mm, t_kept = sem("t_mm"), sem("t_kept")
        stats1, aggr1, var1, rstd1_done = sem("stats1"), sem("aggr1"), sem("var1"), sem("rstd1_done")
        z_done, zt_mm, zt_done = sem("z_done"), sem("zt_mm"), sem("zt_done")
        qkv_mm, v_done, qk_done, vwin_done = sem("qkv_mm"), sem("v_done"), sem("qk_done"), sem("vwin_done")
        tb_done = sem("tb_done")
        scores_mm = [sem(f"scores_mm{g}") for g in range(BANKS)]
        narrow_done = [sem(f"narrow_done{g}") for g in range(BANKS)]
        max_done = [sem(f"max_done{g}") for g in range(BANKS)]
        diff_done = [sem(f"diff_done{g}") for g in range(BANKS)]
        ndiff_done = [sem(f"ndiff_done{g}") for g in range(BANKS)]
        wide_kept = [sem(f"wide_kept{g}") for g in range(BANKS)]
        wmax_done = [sem(f"wmax_done{g}") for g in range(BANKS)]
        exp_done = [sem(f"exp_done{g}") for g in range(BANKS)]
        sum_done = [sem(f"sum_done{g}") for g in range(BANKS)]
        rinv_done = [sem(f"rinv_done{g}") for g in range(BANKS)]
        scaled = [sem(f"scaled{g}") for g in range(BANKS)]
        prob_done = [sem(f"prob_done{g}") for g in range(BANKS)]
        probt_done = [sem(f"probt_done{g}") for g in range(BANKS)]
        pv_mm = [sem(f"pv_mm{g}") for g in range(BANKS)]
        even_done, att_done = sem("even_done"), sem("att_done")
        proj_mm, t2_done = sem("proj_mm"), sem("t2_done")
        stats2, aggr2, var2, rstd2_done = sem("stats2"), sem("aggr2"), sem("var2"), sem("rstd2_done")
        z2_done, z2t_mm, t2b_done = sem("z2_done"), sem("z2t_mm"), sem("t2b_done")
        y_done, yhalf_done, ytiny_done = sem("y_done"), sem("yhalf_done"), sem("ytiny_done")
        tiny8_done, ffn_mm, out_done, out_sent = sem("tiny8_done"), sem("ffn_mm"), sem("out_done"), sem("out_sent")

        def wait(engine, s, units):
            if not (isinstance(units, int) and units <= 0):
                engine.wait_ge(s, units)

        def part(engine):
            engine.wait_ge(zeros_made, 1)

        def on(k, lag, task, *args):
            if not isinstance(k, int) or 0 <= k - lag < UNITS:
                task(k - lag, *args)

        def pipeline(engine, step):
            for k in range(LAST + 1):
                step(k)
            with engine.Fori(LAST + 1, UNITS) as k:
                step(k)
            for k in range(UNITS, UNITS + LAST):
                step(k)

        block = ctx.enter_context(nc.Block())

        @block.sync
        def _(sp):
            sp.dma_start(x_cur[:, :], x[0]).then_inc(x_in, 16)
            sp.dma_start(mask_w[:, :], w_mask).then_inc(gmask_in, 16)
            sp.dma_start(g_w[:, :], w_g).then_inc(gmask_in, 16)
            sp.dma_start(qkv_rows[:, :, :], qkv_w.rearrange("(t o) c -> o t c", t=3)).then_inc(qkv_in, 16)
            sp.dma_start(proj_rows[:, :], proj_w).then_inc(qkv_in, 16)
            sp.dma_start(ffn_k[:, :], ffn_kernel).then_inc(ffn_in, 16)
            sp.dma_start(bias_raw[:, :], ffn_bias.unsqueeze(1)).then_inc(ffn_in, 16)
            sp.dma_start(scales[:, 0:1], input_scale.unsqueeze(0).to_broadcast([C, 1])).then_inc(ffn_in, 16)
            sp.dma_start(scales[:, 1:2], kernel_scale.unsqueeze(0).to_broadcast([C, 1])).then_inc(ffn_in, 16)
            sp.dma_start(proj_bias[:, :], proj_b.unsqueeze(0).to_broadcast([HALF, C])).then_inc(bias_in, 16)

            def load(u):
                sp.wait_ge(t_mm, u)
                sp.dma_start(x_cur[:, :], x[u]).then_inc(x_in, 16)

            def store(u):
                sp.wait_ge(out_done, u + 1)
                sp.dma_start(out[u], out_all[:, u, :]).then_inc(out_sent, 16)

            def step(k):
                if not (isinstance(k, int) and k == 0):
                    on(k, 0, load)
                on(k, 3, store)

            pipeline(sp, step)
            sp.wait_ge(out_sent, 16 * UNITS)

        @block.tensor
        def _(pe):
            mm = nc.tensor.matmul

            pe.wait_ge(bilinear_in, 32)
            mm(bank[0][:, 0:C], theta_w[:, :], phi_w[:, :], start=True, stop=True).then_inc(weight_mm, 1)
            pe.wait_ge(identity_made, 1)
            pe.wait_ge(gmask_in, 32)
            nc.tensor.transpose(bank[1][0:INTER, 0:C], mask_w[:, :], identity[:, :]).then_inc(weight_mm, 1)

            def fold_g_weights():
                pe.wait_ge(weight_done, 2)
                mm(bank[2][:, 0:C], g_w[:, :], mask_wt[:, :], start=True, stop=True).then_inc(weight_mm, 1)

            def turn_weights():
                pe.wait_ge(qkv_in, 32)
                for i in range(3):
                    nc.tensor.transpose(bank[3][:, i * C:(i + 1) * C], qkv_rows[:, i, :], identity[:, :]).then_inc(weight_mm, 1)
                nc.tensor.transpose(bank[3][:, 3 * C:4 * C], proj_rows[:, :], identity[:, :]).then_inc(weight_mm, 1)
                pe.wait_ge(masks_made, 1)
                mm(bank[6][:, 0:KW], query_sel[:, :, :].rearrange("p h q -> p (h q)"), narrow_rows[:, :],
                   start=True, stop=True).then_inc(weight_mm, 1)

            def halves(s):
                return slice(s * HALF, (s + 1) * HALF)

            def apply_bilinear(u):
                if isinstance(u, int) and u == 0:
                    pe.wait_ge(weight_done, 1)
                wait(pe, zt_done, u)
                pe.wait_ge(x_in, 16 * (u + 1))
                mm(ps_u, bilinear_t[:, :], x_cur[:, :], start=True, stop=True).then_inc(u_mm, 1)

            def column_attention(u):
                wait(pe, u_done, u + 1)
                for s in range(2):
                    last = mm(ps_attn, x_cur[:, halves(s)], u_sb[:, halves(s)], start=(s == 0), stop=(s == 1))
                last.then_inc(attn_mm, 1)

            def project_g(u):
                if isinstance(u, int) and u == 0:
                    pe.wait_ge(weight_done, 3)
                for s in range(2):
                    last = mm(ps_g[:, halves(s)], x_cur[:, halves(s)], gmask_t[:, :], start=True, stop=True)
                last.then_inc(g_mm, 1)

            def mix_tokens(u):
                wait(pe, e_done, u + 1)
                wait(pe, g_done, u + 1)
                for s in range(2):
                    mm(ps_t[:, halves(s)], x_cur[:, halves(s)], identity[:, :], start=(s == 0), stop=False,
                       is_transpose=True)
                mm(ps_t, e_sb[:, :], g_sb[:, :], start=False, stop=True).then_inc(t_mm, 1)

            def turn_z(u):
                wait(pe, z_done, u + 1)
                for s in range(2):
                    last = nc.tensor.transpose(ps_zt[:, halves(s)], z_sb[:, halves(s)], identity[:, :])
                last.then_inc(zt_mm, 1)

            def project_qkv(u):
                if isinstance(u, int) and u == 0:
                    pe.wait_ge(weight_done, 4)
                wait(pe, zt_done, u + 1)
                wait(pe, qk_done, u)
                for i, o in ((1, ps_k), (2, ps_v), (0, ps_q)):
                    last = mm(o, qkv_t[:, i, :], zt_sb[:, :], start=True, stop=True)
                last.then_inc(qkv_mm, 1)

            def scores(u, g):
                if g == 0:
                    wait(pe, qk_done, u + 1)
                wait(pe, diff_done[g], u)
                mm(bank[4 + g][:, 0:WB * KW], query_sel[:, :, :].rearrange("p h q -> p (h q)"),
                   wide_mask[:, g * WB:(g + 1) * WB, :].rearrange("p w n -> p (w n)"), start=True, stop=False)
                for w in range(WB):
                    at = (g * WB + w) * QW
                    for i in range(PAIRS):
                        q = slice(QUAD * i, QUAD * (i + 1))
                        last = mm(ps_scores[g][q, w, :],
                                  q_pair[q, g * WB + w, :, :].rearrange("p e q -> p (e q)"),
                                  k_pad[q, at:at + KW], start=False, stop=(w == WB - 1))
                last.then_inc(scores_mm[g], 1)

            def weigh_values(u, g):
                part(pe)
                if g == 0:
                    wait(pe, vwin_done, u + 1)
                    wait(pe, y_done, u)
                    wait(pe, t2b_done, u)
                wait(pe, probt_done[g], u + 1)
                for w in range(WB):
                    at = (g * WB + w) * QUAD
                    for i in range(PAIRS):
                        q = slice(QUAD * i, QUAD * (i + 1))
                        last = mm(ps_pv[q, at:at + QUAD], v_win[q, g * WB + w, :], prob_t[q, g, w, :],
                                  start=True, stop=True)
                last.then_inc(pv_mm[g], 1)

            def project(u):
                if isinstance(u, int) and u == 0:
                    pe.wait_ge(weight_done, 5)
                wait(pe, att_done, u + 1)
                wait(pe, out_done, u)
                a = att_t[:, :, :].rearrange("p w q -> p (w q)")
                for s in range(2):
                    last = mm(ps_proj[:, halves(s)], a[:, halves(s)], proj_t[:, :], start=True, stop=True)
                last.then_inc(proj_mm, 1)

            def turn_back(u):
                wait(pe, z2_done, u + 1)
                for s in range(2):
                    nc.tensor.transpose(ps_z2t[:, halves(s)], z2_sb[:, halves(s)], identity[:, :])
                for s in range(2):
                    last = nc.tensor.transpose(ps_t2t[:, halves(s)], t2_sb[:, halves(s)], identity[:, :])
                last.then_inc(z2t_mm, 1)

            def feed_forward(u):
                part(pe)
                if isinstance(u, int) and u == 0:
                    pe.wait_ge(kernel_done, 3)
                wait(pe, yhalf_done, u + 1)
                wait(pe, tiny8_done, u + 1)
                mm(ps_ffn, kq_twice[:, :], y_half8[:, :], start=True, stop=False)
                mm(ps_ffn, kq[:, :], y_tiny8[:, :], start=False, stop=False)
                mm(ps_ffn, kq_minus[:, :], y_tinyhalf8[:, :], start=False, stop=True).then_inc(ffn_mm, 1)

            def step(k):
                on(k, 0, apply_bilinear)
                if isinstance(k, int) and k == 0:
                    fold_g_weights()
                on(k, 1, project_qkv)
                on(k, 0, column_attention)
                on(k, 3, turn_back)
                on(k, 0, project_g)
                on(k, 1, scores, 0)
                on(k, 0, mix_tokens)
                if isinstance(k, int) and k == 0:
                    turn_weights()
                on(k, 2, weigh_values, 0)
                on(k, 3, feed_forward)
                on(k, 2, weigh_values, 1)
                on(k, 1, scores, 1)
                on(k, 0, turn_z)
                on(k, 2, project)

            pipeline(pe, step)

        @block.scalar
        def _(act):
            act.dma_start(theta_w[:, :], w_theta).then_inc(bilinear_in, 16)
            act.dma_start(phi_w[:, :], w_phi).then_inc(bilinear_in, 16)
            nc.scalar.preload_act_table(ACT.Exp)
            act.wait_ge(weight_mm, 1)
            nc.scalar.copy(bilinear_t[:, :], bank[0][:, 0:C]).then_inc(weight_done, 1)
            act.wait_ge(weight_mm, 2)
            nc.scalar.copy(mask_wt[:, :], bank[1][0:INTER, 0:C]).then_inc(weight_done, 1)

            def copy_g_weights():
                act.wait_ge(weight_mm, 3)
                nc.scalar.copy(gmask_t[:, :], bank[2][:, 0:C]).then_inc(weight_done, 1)

            def copy_weights():
                act.wait_ge(weight_mm, 7)
                nc.scalar.copy(qkv_t[:, :, :].rearrange("p t c -> p (t c)"), bank[3][:, 0:3 * C]).then_inc(weight_done, 1)
                nc.scalar.copy(proj_t[:, :], bank[3][:, 3 * C:4 * C]).then_inc(weight_done, 1)
                act.wait_ge(parity_made, 1)
                act.wait_ge(zeros_made, 1)

            def copy_u(u):
                wait(act, u_mm, u + 1)
                wait(act, attn_mm, u)
                nc.scalar.copy(u_sb[:, :], ps_u).then_inc(u_done, 1)

            def column_exp(u):
                wait(act, nmax_done, u + 1)
                wait(act, t_mm, u)
                nc.scalar.activation(e_sb[:, :], ps_attn, ACT.Exp, bias=col_nmax[:, 0:1], scale=1.0,
                                     accum_out=col_sum[:, 0:1]).then_inc(e_done, 1)

            def scale_g(u):
                wait(act, g_mm, u + 1)
                wait(act, inv_done, u + 1)
                nc.scalar.activation(g_sb[:, :], ps_g, ACT.Copy, scale=col_inv[:, 0:1]).then_inc(g_done, 1)

            def keep_t(u):
                wait(act, t_mm, u + 1)
                wait(act, stats1, u + 1)
                nc.scalar.copy(t_all[:, u, :], ps_t).then_inc(t_kept, 1)

            def copy_zt(u):
                wait(act, zt_mm, u + 1)
                nc.scalar.copy(zt_sb[:, :], ps_zt).then_inc(zt_done, 1)

            def copy_v(u):
                wait(act, qkv_mm, u + 1)
                wait(act, vwin_done, u)
                nc.scalar.mul(v_pad[:, PAD:PAD + TOK], ps_v, 1.0 / KINDS).then_inc(v_done, 1)

            def copy_qk(u):
                wait(act, qkv_mm, u + 1)
                wait(act, scores_mm[1], u)
                nc.scalar.copy(k_pad[:, PAD:PAD + TOK], ps_k)
                for e in range(2):
                    last = nc.scalar.activation(q_pair[:, :, e, :], ps_q.rearrange("p (w q) -> p w q", q=QW),
                                                ACT.Copy, scale=parity_mask[:, e:e + 1])
                last.then_inc(qk_done, 1)

            def keep_scores(u, g):
                wait(act, scores_mm[g], u + 1)
                wait(act, diff_done[g], u)
                wait(act, narrow_done[g], u)
                nc.scalar.copy(wide[:, g].rearrange("p w n -> p (w n)"),
                               ps_scores[g].rearrange("p w n -> p (w n)")).then_inc(wide_kept[g], 1)

            def band_exp(u, g):
                wait(act, diff_done[g], u + 1)
                wait(act, ndiff_done[g], u + 1)
                wait(act, scaled[g], u)
                wait(act, sum_done[g], u)
                nc.scalar.activation(expd[:, g, :], diff[:, g, :], ACT.Exp, scale=SCALE).then_inc(exp_done[g], 1)

            def pick_even(u):
                wait(act, pv_mm[1], u + 1)
                wait(act, att_done, u)
                nc.scalar.activation(att_even[:, :, :],
                                     ps_pv.rearrange("p (w e q) -> p w e q", e=2, q=QW)[:, :, 0, :],
                                     ACT.Copy, scale=parity_mask[:, 0:1]).then_inc(even_done, 1)

            def add_bias(u):
                if isinstance(u, int) and u == 0:
                    act.wait_ge(quant_step, 2)
                wait(act, z2t_mm, u + 1)
                wait(act, y_done, u + 1)
                wait(act, out_done, u)
                nc.scalar.activation(t2b[:, :], ps_t2t, ACT.Identity, bias=bias_col[:, 0:1],
                                     scale=1.0).then_inc(t2b_done, 1)

            def tiny_to_fp8(u):
                part(act)
                wait(act, ytiny_done, u + 1)
                wait(act, ffn_mm, u)
                nc.scalar.activation(y_tiny8[:, :], y_tiny[:, :], ACT.Copy, saturate=False)
                nc.scalar.activation(y_tinyhalf8[:, :], y_tiny[:, :], ACT.Copy, scale=0.5,
                                     saturate=False).then_inc(tiny8_done, 1)

            def step(k):
                on(k, 0, copy_u)
                if isinstance(k, int) and k == 0:
                    copy_g_weights()
                on(k, 1, copy_v)
                on(k, 1, copy_qk)
                on(k, 0, column_exp)
                on(k, 0, scale_g)
                on(k, 3, add_bias)
                on(k, 1, keep_scores, 0)
                on(k, 3, tiny_to_fp8)
                on(k, 0, keep_t)
                if isinstance(k, int) and k == 0:
                    copy_weights()
                on(k, 2, pick_even)
                on(k, 1, keep_scores, 1)
                on(k, 0, copy_zt)
                on(k, 1, band_exp, 0)
                on(k, 1, band_exp, 1)

            pipeline(act, step)

        @block.vector
        def _(dve):
            v = nc.vector
            dve.wait_ge(heads_made, 1)
            v.tensor_reduce(parity_mask[:, :], head_mask[:, :].rearrange("p (i e) -> p e i", e=2),
                            AX.X, ALU.add).then_inc(parity_made, 1)

            def keep_narrow_mask():
                dve.wait_ge(weight_mm, 8)
                v.tensor_copy(narrow_mask[:, :], bank[6][:, 0:KW]).then_inc(mask_kept, 1)

            def quantise_kernel():
                dve.wait_ge(ffn_in, 64)
                v.tensor_copy(bias_bf[:, :], bias_raw[:, :]).then_inc(quant_step, 1)
                dve.wait_ge(quant_step, 1)
                v.tensor_copy(bias_col[:, :], bias_bf[:, :]).then_inc(quant_step, 1)
                v.reciprocal(scale_inv[:, :], scales[:, :]).then_inc(quant_step, 1)
                v.tensor_tensor(scale_prod[:, :], scales[:, 0:1], scales[:, 1:2], ALU.mult).then_inc(quant_step, 1)
                dve.wait_ge(quant_step, 4)
                v.tensor_scalar(ffn_ks[:, :], ffn_k[:, :], scale_inv[:, 1:2], E4M3_MAX, ALU.mult, ALU.min).then_inc(quant_step, 1)
                dve.wait_ge(quant_step, 5)
                v.tensor_scalar(k_half8[:, :], ffn_ks[:, :], -E4M3_MAX, 0.5, ALU.max, ALU.mult, saturate=False).then_inc(quant_step, 1)
                v.tensor_scalar(ffn_kc[:, :], ffn_ks[:, :], TINY, -TINY, ALU.min, ALU.max).then_inc(quant_step, 1)
                dve.wait_ge(quant_step, 7)
                v.tensor_scalar(k_tiny8[:, :], ffn_kc[:, :], 1.0, None, ALU.mult, saturate=False).then_inc(quant_step, 1)
                v.tensor_scalar(k_tinyhalf8[:, :], ffn_kc[:, :], 0.5, None, ALU.mult, saturate=False).then_inc(quant_step, 1)
                dve.wait_ge(quant_step, 9)
                v.scalar_tensor_tensor(k_part[:, 0, :], k_tinyhalf8[:, :], -2.0, k_tiny8[:, :],
                                       ALU.mult, ALU.add).then_inc(quant_step, 1)
                dve.wait_ge(quant_step, 10)
                v.scalar_tensor_tensor(k_part[:, 1, :], k_half8[:, :], 2.0, k_part[:, 0, :],
                                       ALU.mult, ALU.add).then_inc(quant_step, 1)
                dve.wait_ge(quant_step, 11)
                v.tensor_copy(kq[:, :], k_part[:, 1, :]).then_inc(kernel_done, 1)
                v.tensor_scalar(kq_twice[:, :], k_part[:, 1, :], 2.0, None, ALU.mult).then_inc(kernel_done, 1)
                v.tensor_scalar(kq_minus[:, :], k_part[:, 1, :], -2.0, None, ALU.mult).then_inc(kernel_done, 1)

            def halves(s):
                return slice(s * HALF, (s + 1) * HALF)

            def column_max(u):
                wait(dve, attn_mm, u + 1)
                v.tensor_reduce(col_nmax[:, :], ps_attn, AX.X, ALU.max, negate=True).then_inc(nmax_done, 1)

            def column_inverse(u):
                wait(dve, e_done, u + 1)
                wait(dve, g_done, u)
                v.reciprocal(col_inv[:, :], col_sum[:, :]).then_inc(inv_done, 1)

            def stats_first(u):
                wait(dve, t_mm, u + 1)
                v.bn_stats(st1[:, 0, :], ps_t[:, halves(0)])
                v.bn_stats(st1[:, 1, :], ps_t[:, halves(1)]).then_inc(stats1, 1)
                part(dve)
                wait(dve, stats1, u + 1)
                v.bn_aggr(mv1[:, 0, :], st1[:, 0, :])
                v.bn_aggr(mv1[:, 1, :], st1[:, 1, :]).then_inc(aggr1, 1)

            def norm_first(u):
                wait(dve, rstd1_done, u + 1)
                wait(dve, t_kept, u + 1)
                wait(dve, zt_mm, u)
                for s in range(2):
                    last = v.tensor_scalar(z_sb[:, halves(s)], t_all[:, u, halves(s)], mv1[:, s, 0:1],
                                           rstd1[:, s:s + 1], ALU.subtract, ALU.mult)
                last.then_inc(z_done, 1)

            def window_values(u):
                wait(dve, v_done, u + 1)
                wait(dve, pv_mm[1], u)
                windows = bass.AP(v_pad, 0, [[PADDED, C], [QW, WINDOWS], [1, KW]])
                v.transpose(v_win[:, :, :], windows).then_inc(vwin_done, 1)

            def subtract_wide(u, g):
                wait(dve, wide_kept[g], u + 1)
                wait(dve, exp_done[g], u)
                v.tensor_reduce(row_max[:, g, 1, :], wide[:, g], AX.X, ALU.max).then_inc(wmax_done[g], 1)
                wait(dve, wmax_done[g], u + 1)
                v.tensor_tensor(wide_part(diff, g), ps_scores[g],
                                row_max[:, g, 1].unsqueeze(2).to_broadcast([C, WB, KW]),
                                ALU.subtract).then_inc(diff_done[g], 1)

            def narrow_max(u, g):
                wait(dve, narrow_done[g], u + 1)
                wait(dve, ndiff_done[g], u)
                v.tensor_reduce(row_max[:, g, 0, :], narrow[:, g], AX.X, ALU.max).then_inc(max_done[g], 1)

            def row_sums(u, g):
                wait(dve, exp_done[g], u + 1)
                v.tensor_reduce(row_sum[:, g, 1], wide_part(expd, g), AX.X, ALU.add)
                v.tensor_reduce(row_sum[:, g, 0], narrow_part(expd, g), AX.X, ALU.add).then_inc(sum_done[g], 1)
                wait(dve, sum_done[g], u + 1)
                wait(dve, scaled[g], u)
                v.reciprocal(row_inv[:, g], row_sum[:, g]).then_inc(rinv_done[g], 1)

            def turn_probs(u, g):
                wait(dve, prob_done[g], u + 1)
                wait(dve, pv_mm[g], u)
                v.transpose(prob_t[:, g].rearrange("p w n -> p (w n)"),
                            prob[:, g].rearrange("p w n -> p (w n)")).then_inc(probt_done[g], 1)

            def pick_odd(u):
                wait(dve, even_done, u + 1)
                wait(dve, proj_mm, u)
                v.scalar_tensor_tensor(att_t[:, :, :], ps_pv.rearrange("p (w e q) -> p w e q", e=2, q=QW)[:, :, 1, :],
                                       parity_mask[:, 1:2], att_even[:, :, :], ALU.mult, ALU.add).then_inc(att_done, 1)

            def residual(u):
                wait(dve, proj_mm, u + 1)
                wait(dve, tb_done, u + 1)
                wait(dve, z2t_mm, u)
                v.tensor_tensor(t2_sb[:, :], ps_proj, tb_all[:, u, :], ALU.add).then_inc(t2_done, 1)

            def stats_second(u):
                wait(dve, t2_done, u + 1)
                v.bn_stats(st2[:, 0, :], t2_sb[:, halves(0)])
                v.bn_stats(st2[:, 1, :], t2_sb[:, halves(1)]).then_inc(stats2, 1)
                part(dve)
                wait(dve, stats2, u + 1)
                v.bn_aggr(mv2[:, 0, :], st2[:, 0, :])
                v.bn_aggr(mv2[:, 1, :], st2[:, 1, :]).then_inc(aggr2, 1)

            def norm_second(u):
                wait(dve, rstd2_done, u + 1)
                for s in range(2):
                    last = v.tensor_scalar(z2_sb[:, halves(s)], t2_sb[:, halves(s)], mv2[:, s, 0:1],
                                           rstd2[:, s:s + 1], ALU.subtract, ALU.mult)
                last.then_inc(z2_done, 1)

            def quantise(u):
                wait(dve, z2t_mm, u + 1)
                wait(dve, tiny8_done, u)
                wait(dve, ffn_mm, u)
                v.tensor_scalar(y_sb[:, :], ps_z2t, scale_inv[:, 0:1], E4M3_MAX, ALU.mult, ALU.min).then_inc(y_done, 1)
                wait(dve, y_done, u + 1)
                v.tensor_scalar(y_tiny[:, :], y_sb[:, :], TINY, -TINY, ALU.min, ALU.max).then_inc(ytiny_done, 1)
                v.tensor_scalar(y_half8[:, :], y_sb[:, :], -E4M3_MAX, 0.5, ALU.max, ALU.mult,
                                saturate=False).then_inc(yhalf_done, 1)

            def result(u):
                wait(dve, ffn_mm, u + 1)
                wait(dve, t2b_done, u + 1)
                v.scalar_tensor_tensor(out_all[:, u, :], ps_ffn, scale_prod[:, 0:1], t2b[:, :],
                                       ALU.mult, ALU.add).then_inc(out_done, 1)

            def step(k):
                on(k, 0, column_max)
                on(k, 2, row_sums, 1)
                on(k, 0, column_inverse)
                if isinstance(k, int) and k == 0:
                    quantise_kernel()
                on(k, 3, quantise)
                on(k, 2, turn_probs, 0)
                on(k, 2, turn_probs, 1)
                on(k, 0, stats_first)
                if isinstance(k, int) and k == 0:
                    keep_narrow_mask()
                on(k, 3, result)
                on(k, 1, narrow_max, 0)
                on(k, 1, subtract_wide, 0)
                on(k, 0, norm_first)
                on(k, 2, pick_odd)
                on(k, 1, window_values)
                on(k, 1, subtract_wide, 1)
                on(k, 2, residual)
                on(k, 1, narrow_max, 1)
                on(k, 2, stats_second)
                on(k, 1, row_sums, 0)
                on(k, 2, norm_second)

            pipeline(dve, step)

        @block.gpsimd
        def _(pool):
            p = nc.gpsimd

            p.memset(identity[:, :], 0.0).then_inc(pool_const, 1)
            pool.wait_ge(pool_const, 1)
            p.affine_select(out=identity[:, :], in_=identity[:, :], compare_op=ALU.not_equal, fill=1.0, base=0,
                            pattern=[[-1, C]], channel_multiplier=1).then_inc(identity_made, 1)
            p.memset(head_mask[:, :], 1.0).then_inc(pool_const, 1)
            steps = 2
            for sign in (1, -1):
                pool.wait_ge(pool_const, steps)
                p.affine_select(out=head_mask[:, :], in_=head_mask[:, :], compare_op=ALU.is_ge, fill=0.0,
                                base=0 if sign == 1 else D - 1, pattern=[[-sign * D, HEADS]],
                                channel_multiplier=sign).then_inc(pool_const, 1)
                steps += 1
            pool.wait_ge(pool_const, steps)
            p.memset(query_sel[:, :, :], 0.0).then_inc(heads_made, 1)
            pool.wait_ge(heads_made, 1)
            p.affine_select(out=query_sel[:, :, :], in_=query_sel[:, :, :], compare_op=ALU.not_equal, fill=1.0, base=0,
                            pattern=[[0, HEADS], [-1, QW]], channel_multiplier=1).then_inc(pool_const, 1)
            p.memset(wide_mask[:, :, :], 0.0).then_inc(pool_const, 1)
            p.memset(narrow_rows[:, :], 0.0).then_inc(pool_const, 1)
            steps += 3
            pool.wait_ge(pool_const, steps)
            for sign in (1, -1):
                for m, r, pattern in ((narrow_rows[:, :], RADIUS[0], [[sign, KW]]),
                                      (wide_mask[:, :, :], RADIUS[1], [[0, WINDOWS], [sign, KW]])):
                    p.affine_select(out=m, in_=m, compare_op=ALU.is_ge, fill=NEG, base=r - sign * PAD,
                                    pattern=pattern, channel_multiplier=-sign).then_inc(pool_const, 1)
                    steps += 1
                    pool.wait_ge(pool_const, steps)
            m = wide_mask[:, 0, 0:PAD]
            p.memset(m, NEG)
            m = wide_mask[:, WINDOWS - 1, KW - PAD:KW]
            p.memset(m, NEG).then_inc(masks_made, 1)
            p.memset(k_pad[:, 0:PAD], 0.0)
            p.memset(k_pad[:, PAD + TOK:PADDED], 0.0)
            p.memset(v_pad[:, 0:PAD], 0.0)
            p.memset(v_pad[:, PAD + TOK:PADDED], 0.0).then_inc(zeros_made, 1)
            p.memset(minus_half[:, :], -0.5)
            p.memset(ln_eps[:, :], LN_EPS).then_inc(pool_const, 1)
            pool.wait_ge(pool_const, steps + 1)

            def rstd_first(u):
                wait(pool, aggr1, u + 1)
                p.tensor_tensor(ve1[:, :], mv1[:, :, 1], ln_eps[:, :], ALU.add).then_inc(var1, 1)
                wait(pool, var1, u + 1)
                p.tensor_tensor(rstd1[:, :], ve1[:, :], minus_half[:, :], ALU.pow).then_inc(rstd1_done, 1)

            def rstd_second(u):
                wait(pool, aggr2, u + 1)
                p.tensor_tensor(ve2[:, :], mv2[:, :, 1], ln_eps[:, :], ALU.add).then_inc(var2, 1)
                wait(pool, var2, u + 1)
                p.tensor_tensor(rstd2[:, :], ve2[:, :], minus_half[:, :], ALU.pow).then_inc(rstd2_done, 1)

            def add_proj_bias(u):
                if isinstance(u, int) and u == 0:
                    pool.wait_ge(bias_in, 16)
                wait(pool, t_kept, u + 1)
                b = proj_bias[:, :].unsqueeze(1).to_broadcast([HALF, 2, C])
                p.tensor_tensor(tb_all[:, u, :].rearrange("p (s c) -> p s c", s=2),
                                t_all[:, u, :].rearrange("p (s c) -> p s c", s=2), b, ALU.add).then_inc(tb_done, 1)

            def mask_narrow(u, g):
                if isinstance(u, int) and u == 0:
                    pool.wait_ge(mask_kept, 1)
                wait(pool, wide_kept[g], u + 1)
                wait(pool, max_done[g], u)
                wait(pool, ndiff_done[g], u)
                p.tensor_tensor(narrow[:, g], wide[:, g, :, NARROW:NARROW + NW],
                                narrow_mask[:, NARROW:NARROW + NW].unsqueeze(1).to_broadcast([C, WB, NW]), ALU.add).then_inc(narrow_done[g], 1)

            def subtract_narrow(u, g):
                wait(pool, max_done[g], u + 1)
                wait(pool, exp_done[g], u)
                p.tensor_tensor(narrow_part(diff, g), narrow[:, g],
                                row_max[:, g, 0].unsqueeze(2).to_broadcast([C, WB, NW]),
                                ALU.subtract).then_inc(ndiff_done[g], 1)

            def scale_probs(u, g):
                wait(pool, rinv_done[g], u + 1)
                wait(pool, probt_done[g], u)
                p.tensor_tensor(prob[:, g], wide_part(expd, g),
                                row_inv[:, g, 1].unsqueeze(2).to_broadcast([C, WB, KW]), ALU.mult)
                p.tensor_tensor(narrow_prob[:, g], narrow_part(expd, g),
                                row_inv[:, g, 0].unsqueeze(2).to_broadcast([C, WB, NW]), ALU.mult).then_inc(scaled[g], 1)
                wait(pool, scaled[g], u + 1)
                p.tensor_tensor(prob[:, g, :, NARROW:NARROW + NW], prob[:, g, :, NARROW:NARROW + NW],
                                narrow_prob[:, g], ALU.add).then_inc(prob_done[g], 1)

            def step(k):
                on(k, 0, rstd_first)
                on(k, 1, mask_narrow, 1)
                on(k, 0, add_proj_bias)
                on(k, 1, subtract_narrow, 0)
                on(k, 1, subtract_narrow, 1)
                on(k, 2, rstd_second)
                on(k, 1, scale_probs, 0)
                on(k, 1, scale_probs, 1)
                on(k, 0, mask_narrow, 0)

            pipeline(pool, step)


_INS = ['x', 'L0_conv_w_phi', 'L0_conv_w_theta', 'L0_conv_w_g', 'L0_conv_w_mask', 'L1_attn_qkv_w',
        'L1_attn_proj_w', 'L1_attn_proj_b', 'L1_ffn_kernel', 'L1_ffn_bias', 'L1_ffn_input_scale',
        'L1_ffn_kernel_scale']


def kernel(**inputs):
    import numpy as _np
    import concourse.bacc as _bacc
    from concourse import mybir as _mybir
    from concourse.bass_utils import run_bass_kernel_spmd as _run

    nc = _bacc.Bacc("TRN2", target_bir_lowering=False, num_devices=1)
    arrays, args = {}, []
    for name in _INS:
        a = _np.ascontiguousarray(inputs[name])
        shape = a.shape
        if name == 'x':
            a = a.reshape(UNITS, C, TOK)
        arrays[f"in_{name}_dram"] = a
        args.append(nc.dram_tensor(f"in_{name}_dram", a.shape, _mybir.dt.from_np(a.dtype), kind="ExternalInput").ap())
    args.append(nc.dram_tensor("out_0_dram", (UNITS, C, TOK), _mybir.dt.float32, kind="ExternalOutput").ap())
    hybrid_block_kernel(nc, *args)
    r = _run(nc, [arrays], core_ids=[0])
    return _np.asarray(r.results[0]["out_0_dram"]).reshape(UNITS, C, 16, 16)
```
